# Optimizing a Trainium2 kernel written in Bass

```python
import numpy as np
import jax
import jax.numpy as jnp

def _softmax(x, axis=-1):
    return jax.nn.softmax(x, axis=axis)

def _gelu(x):
    return jax.nn.gelu(x, approximate=True)

def _silu(x):
    return jax.nn.silu(x)

def _sigmoid(x):
    return jax.nn.sigmoid(x)

def _layernorm(x, axis=-1, eps=1e-05):
    m = jnp.mean(x, axis=axis, keepdims=True)
    v = jnp.var(x, axis=axis, keepdims=True)
    return (x - m) / jnp.sqrt(v + eps)

def _scatter_add(tgt, idx, src, axis=0):
    return tgt.at[idx].add(src)

def _segment_sum(src, seg, n):
    return jax.ops.segment_sum(src, seg, n)
kernel_name = 'mk_decoder_postln_d1_seqx_r8_79860c'

def setup_inputs(seed: int=0):
    np.random.seed(seed)
    _w = jnp.asarray

    def _rec_inputs():
        import jax
        import jax.numpy as jnp
        _rk = jax.random.key(seed)
        x = -7.109e-05 + 0.9999 * jax.random.normal(jax.random.fold_in(_rk, 1), (16, 56, 512), jnp.float32)
        _lenS = 56 - jax.random.randint(jax.random.fold_in(_rk, 7), (16,), 0, max(1, 56 // 4) + 1, jnp.int32)
        _lenS2 = 1500 - jax.random.randint(jax.random.fold_in(_rk, 8), (16,), 0, max(1, 1500 // 4) + 1, jnp.int32)
        _ctx_4096P = jax.random.normal(jax.random.fold_in(_rk, 11), (16, 16, 512), jnp.float32)
        _ctx_4096c = jax.random.dirichlet(jax.random.fold_in(_rk, 511), 0.3 * jnp.ones((16,), jnp.float32), (16, 1500))
        _ctx_4096t = jnp.einsum('bsk,bkd->bsd', _ctx_4096c, _ctx_4096P)
        _ctx_4096t = _ctx_4096t * jax.lax.rsqrt(jnp.mean(jnp.square(_ctx_4096t)) + 1e-12) * 0.953939
        ctx_4096 = -0.00010331 + 0.999899 * (_ctx_4096t + 0.3 * jax.random.normal(jax.random.fold_in(_rk, 611), (16, 1500, 512), jnp.float32))
        return (x, ctx_4096)
    x, ctx_4096 = _rec_inputs()

    def _L0_attn_setup():
        import jax, jax.numpy as jnp
        import numpy as np
        H_M, P_M, G_M, N_M, K_CONV, CHUNK = (128, 64, 8, 128, 4, 128)
        D_MODEL = 512
        D_INNER = H_M * P_M
        CONV_DIM = D_INNER + 2 * G_M * N_M
        PROJ_DIM = D_INNER + CONV_DIM + H_M
        EPS = 1e-05

        def segsum(x):
            l = x.shape[-1]
            xe = jnp.broadcast_to(x[..., None], x.shape + (l,))
            m1 = jnp.tril(jnp.ones((l, l), dtype=bool), -1)
            s = jnp.cumsum(jnp.where(m1, xe, 0.0), axis=-2)
            m2 = jnp.tril(jnp.ones((l, l), dtype=bool), 0)
            return jnp.where(m2, s, -jnp.inf)

        def causal_conv(x, w, bconv):
            k = w.shape[1]
            s = x.shape[1]
            xp = jnp.pad(x, ((0, 0), (k - 1, 0), (0, 0)))
            y = sum((xp[:, i:i + s, :] * w[:, i] for i in range(k)))
            return y + bconv
        key = jax.random.key(seed)
        ks = jax.random.split(key, 8)
        B_, S = (1, 256)
        sc = 0.02
        return {'x': jax.random.normal(ks[0], (B_, S, D_MODEL), dtype=jnp.float32), 'norm_w': jnp.ones((D_MODEL,), dtype=jnp.float32), 'in_proj_w': jax.random.normal(ks[1], (PROJ_DIM, D_MODEL), dtype=jnp.float32) * sc, 'conv_w': jax.random.normal(ks[2], (CONV_DIM, K_CONV), dtype=jnp.float32) * 0.2, 'conv_b': jnp.zeros((CONV_DIM,), dtype=jnp.float32), 'dt_bias': jax.random.uniform(ks[3], (H_M,), dtype=jnp.float32) * 0.1, 'A_log': jnp.log(1.0 + 15.0 * jax.random.uniform(ks[4], (H_M,), dtype=jnp.float32)), 'Dp': jnp.ones((H_M,), dtype=jnp.float32), 'gnorm_w': jnp.ones((D_INNER,), dtype=jnp.float32), 'out_proj_w': jax.random.normal(ks[5], (D_MODEL, D_INNER), dtype=jnp.float32) * sc}
    _L0_attn_all = _L0_attn_setup()
    _L0_attn_in = {k: v for k, v in _L0_attn_all.items() if k in ('norm_w', 'in_proj_w', 'conv_w', 'conv_b', 'dt_bias', 'A_log', 'Dp', 'gnorm_w', 'out_proj_w')}
    del _L0_attn_all

    def _L0_xattn_setup():
        import jax, jax.numpy as jnp
        import numpy as np
        key = jax.random.key(seed)
        k1, k2 = jax.random.split(key)
        B, Lq, Lk, D = (16, 128, 256, 512)
        query = jax.random.normal(k1, (B, Lq, D), dtype=jnp.float32)
        key_t = jax.random.normal(k2, (B, Lk, D), dtype=jnp.float32)
        return {'query': query, 'key': key_t}
    _L0_xattn_all = _L0_xattn_setup()
    _L0_xattn_in = {k: v for k, v in _L0_xattn_all.items() if k in ()}
    del _L0_xattn_all

    def _L0_ffn_setup():
        import jax, jax.numpy as jnp
        import numpy as np
        B, S, D, O, E, R = (2, 512, 512, 512, 8, 16)
        TOP_K = 2
        SCALING = 32.0 / 16.0
        key = jax.random.key(seed)
        k = jax.random.split(key, 6)
        x = jax.random.normal(k[0], (B, S, D), dtype=jnp.float32)
        W_base = jax.random.normal(k[1], (O, D), dtype=jnp.float32) * 0.02
        b_base = jax.random.normal(k[2], (O,), dtype=jnp.float32) * 0.02
        W_router = jax.random.normal(k[3], (E, D), dtype=jnp.float32) * 0.01
        lora_A = jax.random.normal(k[4], (E, R, D), dtype=jnp.float32) * (1.0 / np.sqrt(D))
        lora_B = jax.random.normal(k[5], (E, O, R), dtype=jnp.float32) * 0.02
        return {'x': x, 'W_base': W_base, 'b_base': b_base, 'W_router': W_router, 'lora_A': lora_A, 'lora_B': lora_B}
    _L0_ffn_all = _L0_ffn_setup()
    _L0_ffn_in = {k: v for k, v in _L0_ffn_all.items() if k in ('W_base', 'b_base', 'W_router', 'lora_A', 'lora_B')}
    del _L0_ffn_all
    return {'x': x, 'ctx_4096': ctx_4096, 'L0_attn_norm_w': _L0_attn_in['norm_w'], 'L0_attn_in_proj_w': _L0_attn_in['in_proj_w'], 'L0_attn_conv_w': _L0_attn_in['conv_w'], 'L0_attn_conv_b': _L0_attn_in['conv_b'], 'L0_attn_dt_bias': _L0_attn_in['dt_bias'], 'L0_attn_A_log': _L0_attn_in['A_log'], 'L0_attn_Dp': _L0_attn_in['Dp'], 'L0_attn_gnorm_w': _L0_attn_in['gnorm_w'], 'L0_attn_out_proj_w': _L0_attn_in['out_proj_w'], 'L0_ffn_W_base': _L0_ffn_in['W_base'], 'L0_ffn_b_base': _L0_ffn_in['b_base'], 'L0_ffn_W_router': _L0_ffn_in['W_router'], 'L0_ffn_lora_A': _L0_ffn_in['lora_A'], 'L0_ffn_lora_B': _L0_ffn_in['lora_B']}

def reference(x, ctx_4096, L0_attn_norm_w, L0_attn_in_proj_w, L0_attn_conv_w, L0_attn_conv_b, L0_attn_dt_bias, L0_attn_A_log, L0_attn_Dp, L0_attn_gnorm_w, L0_attn_out_proj_w, L0_ffn_W_base, L0_ffn_b_base, L0_ffn_W_router, L0_ffn_lora_A, L0_ffn_lora_B):
    import jax
    import jax.numpy as jnp

    def _L0_attn_ref(x, norm_w, in_proj_w, conv_w, conv_b, dt_bias, A_log, Dp, gnorm_w, out_proj_w):
        import jax, jax.numpy as jnp
        import numpy as np
        H_M, P_M, G_M, N_M, K_CONV, CHUNK = (128, 64, 8, 128, 4, 128)
        D_MODEL = 512
        D_INNER = H_M * P_M
        CONV_DIM = D_INNER + 2 * G_M * N_M
        PROJ_DIM = D_INNER + CONV_DIM + H_M
        EPS = 1e-05

        def segsum(x):
            l = x.shape[-1]
            xe = jnp.broadcast_to(x[..., None], x.shape + (l,))
            m1 = jnp.tril(jnp.ones((l, l), dtype=bool), -1)
            s = jnp.cumsum(jnp.where(m1, xe, 0.0), axis=-2)
            m2 = jnp.tril(jnp.ones((l, l), dtype=bool), 0)
            return jnp.where(m2, s, -jnp.inf)

        def causal_conv(x, w, bconv):
            k = w.shape[1]
            s = x.shape[1]
            xp = jnp.pad(x, ((0, 0), (k - 1, 0), (0, 0)))
            y = sum((xp[:, i:i + s, :] * w[:, i] for i in range(k)))
            return y + bconv
        b, s, _ = x.shape
        residual = x
        h = x * jax.lax.rsqrt(jnp.mean(x * x, axis=-1, keepdims=True) + EPS) * norm_w
        proj = jnp.einsum('bsd,od->bso', h, in_proj_w)
        gate = proj[..., :D_INNER]
        hBC = proj[..., D_INNER:D_INNER + CONV_DIM]
        dt = proj[..., D_INNER + CONV_DIM:]
        hBC = jax.nn.silu(causal_conv(hBC, conv_w, conv_b))
        hid = hBC[..., :D_INNER].reshape(b, s, H_M, P_M)
        B = hBC[..., D_INNER:D_INNER + G_M * N_M].reshape(b, s, G_M, N_M)
        C = hBC[..., D_INNER + G_M * N_M:].reshape(b, s, G_M, N_M)
        dt = jax.nn.softplus(dt + dt_bias)
        A = -jnp.exp(A_log)
        pad = -s % CHUNK
        D_res = Dp[None, None, :, None] * hid
        hid_dt = hid * dt[..., None]
        A_full = A[None, None, :] * dt

        def padseq(t):
            return jnp.pad(t, [(0, 0), (0, pad)] + [(0, 0)] * (t.ndim - 2))
        hid_dt, A_full, Bp, Cp = (padseq(hid_dt), padseq(A_full), padseq(B), padseq(C))
        S = s + pad
        c, l = (S // CHUNK, CHUNK)
        hc = hid_dt.reshape(b, c, l, H_M, P_M)
        Ac = A_full.reshape(b, c, l, H_M).transpose(0, 3, 1, 2)
        rep = H_M // G_M
        Bh = jnp.repeat(Bp.reshape(b, c, l, G_M, N_M), rep, axis=3)
        Ch = jnp.repeat(Cp.reshape(b, c, l, G_M, N_M), rep, axis=3)
        A_cs = jnp.cumsum(Ac, axis=-1)
        L = jnp.exp(segsum(Ac))
        M = jnp.einsum('bcihn,bcjhn->bcijh', Ch, Bh) * jnp.transpose(L, (0, 2, 3, 4, 1))
        Y_diag = jnp.einsum('bcijh,bcjhp->bcihp', M, hc)
        decay_states = jnp.exp(A_cs[..., -1:] - A_cs)
        states = jnp.einsum('bclhn,bhcl,bclhp->bchpn', Bh, decay_states, hc)
        A_last = jnp.pad(A_cs[..., -1], ((0, 0), (0, 0), (1, 0)))
        decay_chunk = jnp.exp(segsum(A_last))
        states_cat = jnp.concatenate([jnp.zeros_like(states[:, :1]), states], axis=1)
        prev_states = jnp.einsum('bhij,bjhpn->bihpn', decay_chunk, states_cat)[:, :-1]
        Y_off = jnp.einsum('bclhn,bchpn,bhcl->bclhp', Ch, prev_states, jnp.exp(A_cs))
        y = (Y_diag + Y_off).reshape(b, S, H_M, P_M)[:, :s] + D_res
        y = y.reshape(b, s, D_INNER)
        yg = y * jax.nn.silu(gate)
        gsz = D_INNER // G_M
        ygr = yg.reshape(b, s, G_M, gsz)
        ygr = ygr * jax.lax.rsqrt(jnp.mean(ygr * ygr, axis=-1, keepdims=True) + EPS)
        y = ygr.reshape(b, s, D_INNER) * gnorm_w
        out = jnp.einsum('bsd,od->bso', y, out_proj_w)
        return residual + out

    def _L0_xattn_ref(query, key):
        import jax, jax.numpy as jnp
        import numpy as np
        a = jnp.einsum('bqd,bkd->bqk', query, key)
        e = jax.nn.softmax(a, axis=-1)
        c = jnp.einsum('bqk,bkd->bqd', e, key)
        return c

    def _L0_ffn_ref(x, W_base, b_base, W_router, lora_A, lora_B):
        import jax, jax.numpy as jnp
        import numpy as np
        B, S, D, O, E, R = (2, 512, 512, 512, 8, 16)
        TOP_K = 2
        SCALING = 32.0 / 16.0
        d = x.shape[-1]
        n_experts = W_router.shape[0]
        xf = x.reshape(-1, d)
        logits = xf @ W_router.T
        probs = jax.nn.softmax(logits, axis=-1)
        topk_p, topk_i = jax.lax.top_k(probs, TOP_K)
        topk_p = topk_p / jnp.sum(topk_p, axis=-1, keepdims=True)
        w = jnp.sum(jax.nn.one_hot(topk_i, n_experts, dtype=xf.dtype) * topk_p[..., None], axis=1)
        h = jnp.einsum('td,erd->ter', xf, lora_A)
        lora_out = jnp.einsum('ter,eor,te->to', h, lora_B, w) * SCALING
        base = x @ W_base.T + b_base
        return base + lora_out.reshape(x.shape[:-1] + (W_base.shape[0],))
    x = _layernorm(x + _L0_attn_ref(x, L0_attn_norm_w, L0_attn_in_proj_w, L0_attn_conv_w, L0_attn_conv_b, L0_attn_dt_bias, L0_attn_A_log, L0_attn_Dp, L0_attn_gnorm_w, L0_attn_out_proj_w), axis=-1)
    x = _layernorm(x + _L0_xattn_ref(x, ctx_4096), axis=-1)
    x = _layernorm(x + _L0_ffn_ref(x, L0_ffn_W_base, L0_ffn_b_base, L0_ffn_W_router, L0_ffn_lora_A, L0_ffn_lora_B), axis=-1)
    return x

_drawn_inputs = setup_inputs


def setup_inputs(seed=0):
    import zlib

    import numpy as np

    out = dict(_drawn_inputs(seed))
    spreads = {'L0_attn_norm_w': (1.0, 0.2),
     'L0_attn_conv_b': (0.0, 0.1),
     'L0_attn_Dp': (1.0, 0.2),
     'L0_attn_gnorm_w': (1.0, 0.2)}
    factors = {'L0_attn_dt_bias': 8.0, 'L0_ffn_b_base': 3.174}
    for name, (base, spread) in spreads.items():
        noise = np.random.default_rng([zlib.crc32(name.encode()), seed]).standard_normal(out[name].shape)
        drawn = base * np.exp(spread * noise) if base else spread * noise
        out[name] = jnp.asarray(drawn.astype(out[name].dtype))
    for name, factor in factors.items():
        out[name] = (out[name] * factor).astype(out[name].dtype)
    return out
```

```python
import concourse.bass as bass
from concourse import mybir
from contextlib import ExitStack

f32 = mybir.dt.float32
f32r = mybir.dt.float32r
ALU = mybir.AluOpType
ACT = mybir.ActivationFunctionType
AX = mybir.AxisListType

P = 128
SEQS, LEN, DM = 16, 56, 512
TOK = SEQS * LEN
PAD = 64
PAIRS = SEQS // 2
HALF = TOK // 2
KT = DM // P
TT = TOK // P
GROUPS, HEADS, HD = 8, 128, 64
CT = 8
WT = 2 + 2 * CT
TAPS = 4
KEYS = 1500
KJ, KP = 12, 125
EXP, RANK = 8, 16
RMS_EPS = 1e-5
LN_EPS = 1e-5
LORA_SCALE = 2.0


def bc(ap, axis, n):
    v = ap.unsqueeze(axis)
    shape = list(v.shape)
    shape[axis] = n
    return v.broadcast_to(shape)


def layer_kernel(nc, A):
    ctx = ExitStack()
    with ctx:
        def sb(name, shape, dt=f32, stack=ctx):
            return stack.enter_context(nc.sbuf_tensor(name, shape, dt))

        def pb(name, shape):
            return ctx.enter_context(nc.psum_tensor(name, shape, f32))

        def sem(name):
            return ctx.enter_context(nc.semaphore(name))

        acc = sb("acc", [P, TT, DM])
        ident = sb("ident", [P, P])
        ones = sb("ones", [P, 1])
        epsc = sb("epsc", [P, TT])
        stats = sb("stats", [P, 6])
        mv1 = sb("mv1", [P, TT, 2])
        var1 = sb("var1", [P, TT])
        rstd1 = sb("rstd1", [P, TT])

        mix = ExitStack()
        h_hi = sb("h_hi", [P, KT, TOK], f32r, mix)
        h_lo = sb("h_lo", [P, KT, TOK], f32r, mix)
        w_raw = sb("w_raw", [P, 3, KT * P], f32, mix)
        w_hi = sb("w_hi", [P, 3, KT * P], f32r, mix)
        w_lo = sb("w_lo", [P, 3, KT * P], f32r, mix)
        wo_raw = sb("wo_raw", [P, 2, DM], f32, mix)
        wo_hi = sb("wo_hi", [P, 4, DM], f32r, mix)
        wo_lo = sb("wo_lo", [P, 4, DM], f32r, mix)
        decay = sb("decay", [P, 4, TOK], f32, mix)
        mixw = sb("mixw", [P, 2, PAIRS, 2 * LEN], f32, mix)
        hd_dt = sb("hd_dt", [P, PAIRS, P], f32, mix)
        conv = sb("conv", [P, 2, TOK], f32, mix)
        hid = sb("hid", [P, 2, SEQS * PAD], f32, mix)
        gate = sb("gate", [P, 2, TOK], f32, mix)
        bmat = sb("bmat", [P, SEQS * PAD], f32, mix)
        cmat = sb("cmat", [P, SEQS * PAD], f32, mix)
        cbm = sb("cbm", [P, PAIRS, LEN], f32, mix)
        yg = sb("yg", [P, 2, TOK], f32, mix)
        y_hi = sb("y_hi", [P, 4, TOK], f32r, mix)
        y_lo = sb("y_lo", [P, 4, TOK], f32r, mix)
        sq = sb("sq", [P, TOK], f32, mix)
        sqsum = sb("sqsum", [P, TOK], f32, mix)
        part = sb("part", [P, TT, DM], f32, mix)
        cs_j = sb("cs_j", [P, PAIRS, HEADS], f32, mix)
        dt_j = sb("dt_j", [P, PAIRS, HEADS], f32, mix)
        conv_w = sb("conv_w", [P, 80, TAPS], f32, mix)
        conv_b = sb("conv_b", [P, 80], f32, mix)
        skip = sb("skip", [P, GROUPS * CT], f32, mix)
        gnorm = sb("gnorm", [P, GROUPS * CT], f32, mix)
        norm_w = sb("norm_w", [P, KT], f32, mix)
        dt_bias = sb("dt_bias", [P, 1], f32, mix)
        a_log = sb("a_log", [P, 1], f32, mix)
        a_exp = sb("a_exp", [P, 1], f32, mix)
        causal = sb("causal", [P, LEN], f32, mix)
        causal_hi = sb("causal_hi", [P, LEN], f32, mix)
        ssq0 = sb("ssq0", [P, TT], f32, mix)
        ms0 = sb("ms0", [P, TT], f32, mix)
        r0 = sb("r0", [P, TT], f32, mix)
        ms = sb("ms", [P, TT], f32, mix)
        rg = sb("rg", [P, TT], f32, mix)
        mix.close()

        att = ExitStack()
        keys = sb("keys", [P, 2, 2, KJ, DM], f32, att)
        keysT = sb("keysT", [P, 2, 2, KEYS], f32, att)
        x1p = sb("x1p", [P, 2, DM], f32, att)
        qT = sb("qT", [P, KT, P], f32, att)
        probs = sb("probs", [P, KEYS], f32, att)
        probsT = sb("probsT", [P, KJ, P], f32, att)
        x2 = sb("x2", [P, 2, DM], f32, att)
        x2T = sb("x2T", [P, KT, P], f32, att)
        wbT = sb("wbT", [P, KT, DM], f32, att)
        waT = sb("waT", [P, KT, P + EXP], f32, att)
        wlb = sb("wlb", [P, DM], f32, att)
        bias = sb("bias", [P, DM], f32, att)
        z3 = sb("z3", [P, 2, DM], f32, att)
        hw = sb("hw", [P, P], f32, att)
        hwT = sb("hwT", [P, P], f32, att)
        order = sb("order", [P, EXP], f32, att)
        smalls = {n: sb("s_" + n, [P, k], f32, att) for n, k in dict(
            nmax=1, esum=1, rsum=1, mv2=2, var2=1, rstd2=1, mv3=2, var3=1, rstd3=1,
            lg=8, nlm=1, le=8, lsum=1, lr=1, pr=8, v1=1, k1=8, km1=1, oh1=8, p2=8, v2=1, k2=8, km2=1,
            oh2=8, sel=8, top=8, tsum=1, tr=1, wgt=8, st2=6, st3=6).items()}
        S = {k: v[:] for k, v in smalls.items()}
        att.close()

        bank = pb("bank", [P, 8, 512])
        proj = [bank[:, 0:2, :], bank[:, 2:4, :]]
        yt = bank[:, 4:6, :]
        ob = bank[:, 6:8, :]
        scores = bank[:, 0:3, 0:KEYS // 3]
        kt_bank = [bank[:, 3, :], bank[:, 4, :]]
        pv = bank[:, 5, :]
        ffn = bank[:, 6, :]
        misc = bank[:, 7, :]

        cs_dram = nc.dram_tensor("cs_scratch", (2, HEADS, PAIRS, LEN), f32).ap()
        x1_dram = nc.dram_tensor("x1_scratch", (TOK, DM), f32).ap()

        names = """x_loaded params_loaded dtw_loaded consts_set pool_step sqs_done ms0_set r0_set h_scaled
            hT_done h_evac_hi h_evac_lo dtw_hi dtw_lo dt_proj dt_act dt_dve cs_stored cst_done cst_evac
            w_high w_low w_used tap0_done conv_tap silu_done gate_done t_done hd_done y_done yres_done
            p_done y_high y_low sq_done sqsum_done d_done abs_done exp_done m_lo_done m_hi_done cb_done cbm_done
            ss_done ms_done rg_done outa_done outa_evac outb_done psum_added sum_done
            wo_high wo_low zeroed
            xres_loaded ln1_step ln1_var ln1_rstd x1_set x1_stored ffn_loaded order_set
            q_tr q_evac k_tr kev_act kev_dve s_mm nmax_done exps_done rsum_done pT_tr pT_evac pv_done
            z2_done var2_done rstd2_done x2_done x2_tr x2_evac base_done route_done lg_done le_done
            stats_set hw_done hw_tr hw_evac ffn_done z3_done var3_done rstd3_done out_ready dstep""".split()
        s = {n: sem(n) for n in names}
        w_loaded = [sem(f"w_loaded{i}") for i in range(3)]
        wo_loaded = [sem(f"wo_loaded{i}") for i in range(2)]
        cs_loaded = [sem(f"cs_loaded{i}") for i in range(4)]
        keys_loaded = [sem(f"keys_loaded{i}") for i in range(2)]
        x1_loaded = [sem(f"x1_loaded{i}") for i in range(2)]
        stored = [sem(f"stored{i}") for i in range(2)]

        def wait(eng, semaphore, per, g, k):
            if isinstance(g, int):
                if per * g + k > 0:
                    eng.wait_ge(semaphore, per * g + k)
            else:
                eng.wait_ge(semaphore, g * per + k)

        def within(g, c):
            return not isinstance(g, int) or 0 <= g * CT + c < GROUPS * CT

        def has_group(g):
            return not isinstance(g, int) or g < GROUPS

        def w_exists(g, idx):
            return not isinstance(g, int) or g * WT + idx < GROUPS * WT

        def seqs(ap):
            return ap.rearrange("p (b i) -> p b i", b=SEQS)

        def bank_seqs(t):
            return t.rearrange("p h (b i) -> p (h b) i", i=PAD)[:, :, 0:LEN]

        def real(ap):
            return ap.rearrange("p (b i) -> p b i", b=SEQS)[:, :, 0:LEN]

        block = ctx.enter_context(nc.Block())

        def over_groups(eng, body):
            body(0)
            with eng.Fori(1, GROUPS - 1) as g:
                body(g)
            body(GROUPS - 1)

        def over_pairs(eng, body):
            body(0)
            body(1)
            with eng.Fori(2, PAIRS // 2) as n:
                body(n)

        def pair_exists(n, u):
            return not isinstance(n, int) or 2 * n + u >= 0

        @block.sync
        def _(sp):
            sp.dma_start(part[:], A["x"].rearrange("(t p) d -> p t d", p=P)).then_inc(s["x_loaded"], 16)
            sp.dma_start(wo_raw[:, 0, :], A["w_dt"]).then_inc(s["dtw_loaded"], 16)
            for dst, src in ((norm_w[:], A["norm_w"]), (dt_bias[:], A["dt_bias"]), (a_log[:], A["a_log"]),
                             (conv_w[:], A["conv_w"].rearrange("p (t k) -> p t k", k=TAPS)),
                             (conv_b[:], A["conv_b"]), (gnorm[:], A["gnorm"]),
                             (skip[0:HD, :], A["skip"][0:1, :].broadcast_to([HD, GROUPS * CT])),
                             (skip[HD:P, :], A["skip"][1:2, :].broadcast_to([HD, GROUPS * CT]))):
                sp.dma_start(dst, src).then_inc(s["params_loaded"], 16)

            def load_w(g, idx):
                if not w_exists(g, idx):
                    return
                wait(sp, s["w_low"], WT, g, idx - 2)
                sp.dma_start(w_raw[:, idx % 3, :], A["w_in"][g * WT + idx, :, :]
                             ).then_inc(w_loaded[idx % 3], 16)

            def load_wo(g, c):
                if not within(g, c):
                    return
                wait(sp, s["wo_low"], CT, g, c - 1)
                if isinstance(g, int) and g == 0 and c == 0:
                    sp.wait_ge(s["dtw_lo"], 1)
                sp.dma_start(wo_raw[:, c % 2, :], A["w_out"][g * CT + c, :, :]).then_inc(wo_loaded[c % 2], 16)

            def load_cs(g, c):
                if not within(g, c):
                    return
                wait(sp, s["m_lo_done"], CT, g, c - 3)
                wait(sp, s["m_hi_done"], CT, g, c - 3)
                for half in range(2):
                    src = cs_dram[half, bass.ds(g * 16 + 2 * c, 2), :, :].rearrange("h p i -> (h p i)")
                    sp.dma_start(decay[PAD * half:PAD * half + LEN, c % 4, :],
                                 src.unsqueeze(0).broadcast_to([LEN, TOK])).then_inc(cs_loaded[c % 4], 16)

            for idx in range(4):
                load_w(0, idx)
            sp.wait_ge(s["dt_dve"], 5)
            for half in range(2):
                sp.dma_start(cs_dram[half].rearrange("h p i -> h p i"),
                             hid[:, 0, :].rearrange("h (p two i) -> h p two i", two=2, i=PAD)[:, :, half, 0:LEN]
                             ).then_inc(s["cs_stored"], 16)
            sp.wait_ge(s["cs_stored"], 32)
            sp.wait_ge(s["zeroed"], 1)
            for c in range(3):
                load_cs(0, c)

            def group(g):
                for st in range(CT):
                    if st == 0:
                        load_w(g, 4)
                        load_w(g, 5)
                    load_cs(g, st + 3)
                    load_w(g, 6 + 2 * st)
                    load_w(g, 7 + 2 * st)
                    load_wo(g, st)
            over_groups(sp, group)

            sp.wait_ge(s["m_lo_done"], GROUPS * CT)
            sp.wait_ge(s["m_hi_done"], GROUPS * CT)
            sp.dma_start(decay[:].rearrange("p a n -> p (a n)").rearrange("p (t d) -> p t d", t=TT),
                         A["x"].rearrange("(t p) d -> p t d", p=P)).then_inc(s["xres_loaded"], 16)
            sp.wait_ge(s["sum_done"], GROUPS * TT)
            sp.wait_ge(s["ln1_step"], 3 * TT)

            def load_keys(n, u):
                for q in range(2):
                    for lo, hi in ((0, 112), (112, KP)):
                        sp.dma_start(keys[lo:hi, u, q].rearrange("p j d -> p (j d)"),
                                     A["context"][n * 4 + 2 * u + q, lo:hi, :]).then_inc(keys_loaded[u], 16)

            def load_x1(n, u):
                for q in range(2):
                    sp.dma_start(x1p[PAD * q:PAD * q + LEN, u, :],
                                 x1_dram[bass.ds(n * 4 * LEN + (2 * u + q) * LEN, LEN), :]).then_inc(x1_loaded[u], 16)

            def store(n, u):
                wait(sp, s["out_ready"], 2, n, u + 1)
                for q in range(2):
                    sp.dma_start(A["out"][bass.ds(n * 4 * LEN + (2 * u + q) * LEN, LEN), :],
                                 z3[PAD * q:PAD * q + LEN, u % 2, :]).then_inc(stored[u % 2], 16)

            load_keys(0, 0)
            for dst, src in ((wbT[:], A["w_base"].rearrange("p (k n) -> p k n", k=KT)),
                             (waT[:], A["w_a"].rearrange("p (k n) -> p k n", k=KT)),
                             (wlb[:], A["w_b"]),
                             (bias[:], A["b_base"].broadcast_to([P, DM]))):
                sp.dma_start(dst, src).then_inc(s["ffn_loaded"], 16)
            for t in range(TT):
                sp.wait_ge(s["x1_set"], t + 1)
                sp.dma_start(x1_dram[t * P:(t + 1) * P, :], acc[:, t, :]).then_inc(s["x1_stored"], 16)
            sp.wait_ge(s["x1_stored"], 16 * TT)
            sp.wait_ge(s["order_set"], 2)
            load_x1(0, 0)
            load_keys(0, 1)
            load_x1(0, 1)

            def pairs(n, more=True):
                for u in range(2):
                    if pair_exists(n, u - 2):
                        store(n, u - 2)
                    if more:
                        wait(sp, s["pv_done"], 2, n, u + 1)
                        load_keys(n + 1, u)
                    if more:
                        wait(sp, s["z2_done"], 2, n, u + 1)
                        load_x1(n + 1, u)
            pairs(0)
            with sp.Fori(1, PAIRS // 2 - 1) as n:
                pairs(n)
            pairs(PAIRS // 2 - 1, more=False)
            store(PAIRS // 2, -2)
            store(PAIRS // 2, -1)
            for i in range(2):
                sp.wait_ge(stored[i], 32 * PAIRS // 2)

        @block.gpsimd
        def _(pool):
            def take(name):
                pool.wait_ge(s[name], 1)
                pool.sem_inc(s[name], -1)

            g_ = nc.gpsimd
            g_.memset(ones[:], 1.0)
            g_.memset(epsc[:], -0.5)
            g_.memset(ident[:], 0.0).then_inc(s["pool_step"], 1)
            g_.memset(causal[:], 1.0)
            g_.memset(causal_hi[:], 1.0).then_inc(s["pool_step"], 1)
            pool.wait_ge(s["pool_step"], 2)
            g_.affine_select(out=ident[:], in_=ident[:], compare_op=ALU.not_equal, fill=1.0, base=0,
                             pattern=[[-1, P]], channel_multiplier=1)
            for mask, base in ((causal, 0), (causal_hi, PAD)):
                last = g_.affine_select(out=mask[:], in_=mask[:], compare_op=ALU.is_ge, fill=0.0, base=base,
                                        pattern=[[1, LEN]], channel_multiplier=-1)
            last.then_inc(s["consts_set"], 1)
            g_.memset(decay[:].rearrange("p a n -> p (a n)"), 0.0)
            g_.memset(mixw[:].rearrange("p a b n -> p (a b n)"), 0.0)
            g_.memset(bmat[:], 0.0)
            g_.memset(cmat[:], 0.0)
            g_.memset(acc[:].rearrange("p t d -> p (t d)"), 0.0).then_inc(s["zeroed"], 1)
            take("ms0_set")
            g_.tensor_tensor(r0[:], ms0[:], epsc[:], ALU.pow).then_inc(s["r0_set"], 1)

            def split_low(g, idx):
                if not w_exists(g, idx):
                    return
                wait(pool, s["w_high"], WT, g, idx + 1)
                wait(pool, s["w_used"], WT, g, idx - 2)
                g_.tensor_tensor(out=w_lo[:, idx % 3, :], in0=w_raw[:, idx % 3, :], in1=w_hi[:, idx % 3, :].bitcast(f32), op=ALU.subtract).then_inc(s["w_low"], 1)

            pool.wait_ge(s["dtw_hi"], 1)
            g_.tensor_tensor(out=wo_lo[:, 0, :], in0=wo_raw[:, 0, :], in1=wo_hi[:, 0, :].bitcast(f32), op=ALU.subtract).then_inc(s["dtw_lo"], 1)
            split_low(0, 0)
            split_low(0, 1)

            def y_low(g, c):
                if not within(g, c):
                    return
                wait(pool, s["y_high"], CT, g, c + 1)
                g_.tensor_tensor(out=y_lo[:, c % 4, :], in0=yg[:, c % 2, :], in1=y_hi[:, c % 4, :].bitcast(f32), op=ALU.subtract).then_inc(s["y_low"], 1)

            def add_squares(g, c):
                if not within(g, c) or c % CT == 0:
                    return
                wait(pool, s["sq_done"], 7, g, c if c > 0 else c + 1)
                g_.tensor_tensor(out=sqsum[:], in0=sq[:], in1=sqsum[:], op=ALU.add).then_inc(s["sqsum_done"], 1)

            def mix_low(g, c):
                if not within(g, c):
                    return
                wait(pool, s["exp_done"], CT, g, c + 1)
                wait(pool, s["y_done"], CT, g, c)
                wait(pool, s["cbm_done"], 1, g, 1 if c >= 0 else 0)
                g_.tensor_tensor(
                    out=mixw[0:PAD, :, :, 0:LEN],
                    in0=decay[0:PAD, c % 4, :].rearrange("p (h q i) -> p h q i", h=2, i=LEN), in1=bc(cbm[0:PAD, :, :], 1, 2), op=ALU.mult).then_inc(s["m_lo_done"], 1)

            def group_rms(g):
                take("ms_done")
                g_.tensor_tensor(rg[:], ms[:], epsc[:], ALU.pow).then_inc(s["rg_done"], 1)

            def group(g, steps=CT):
                for st in range(steps):
                    mix_low(g, st - 1)
                    if st == 0:
                        split_low(g, 2)
                    y_low(g, st - 2)
                    if st == 0:
                        split_low(g, 3)
                    split_low(g, 4 + 2 * st)
                    add_squares(g, st - 2)
                    split_low(g, 5 + 2 * st)
                    if st == 1 and not (isinstance(g, int) and g == 0):
                        group_rms(g)
            over_groups(pool, group)
            group(GROUPS, 2)

            pool.wait_ge(s["ln1_var"], 1)
            g_.tensor_tensor(rstd1[:], var1[:], epsc[:], ALU.pow).then_inc(s["ln1_rstd"], 1)
            pool.wait_ge(s["ln1_step"], 3 * TT)
            g_.memset(x1p[:].rearrange("p a d -> p (a d)"), 0.0).then_inc(s["order_set"], 1)
            for e in range(EXP):
                last = g_.memset(order[:, e:e + 1], float(EXP - e))
            last.then_inc(s["order_set"], 1)

            def rstd2(n, u):
                if not pair_exists(n, u):
                    return
                wait(pool, s["var2_done"], 2, n, u + 1)
                g_.tensor_tensor(S["rstd2"], S["var2"], epsc[:, 0:1], ALU.pow).then_inc(s["rstd2_done"], 1)

            def rstd3(n, u):
                if not pair_exists(n, u):
                    return
                wait(pool, s["var3_done"], 2, n, u + 1)
                g_.tensor_tensor(S["rstd3"], S["var3"], epsc[:, 0:1], ALU.pow).then_inc(s["rstd3_done"], 1)

            def pairs(n):
                for u in range(2):
                    rstd2(n, u - 1)
                    rstd3(n, u - 2)
            over_pairs(pool, pairs)
            rstd2(PAIRS // 2, -1)
            rstd3(PAIRS // 2, -2)
            rstd3(PAIRS // 2, -1)

        @block.scalar
        def _(act):
            a = nc.scalar.activation
            act.wait_ge(s["x_loaded"], 16)
            for t in range(TT):
                if t:
                    act.wait_ge(s["sqs_done"], t)
                a(sq[:, 0:DM], part[:, t, :], ACT.Square, accum_out=ssq0[:, t:t + 1]).then_inc(s["sqs_done"], 1)
            act.wait_ge(s["params_loaded"], 16 * 8)
            act.wait_ge(s["dtw_loaded"], 16)
            a(wo_hi[:, 0, :], wo_raw[:, 0, :], ACT.Copy).then_inc(s["dtw_hi"], 1)

            def split_high(g, idx):
                if not w_exists(g, idx):
                    return
                wait(act, w_loaded[idx % 3], 16 * (WT // 3), g, 16 * (idx // 3 + 1))
                wait(act, s["w_used"], WT, g, idx - 2)
                a(w_hi[:, idx % 3, :], w_raw[:, idx % 3, :], ACT.Copy).then_inc(s["w_high"], 1)

            split_high(0, 0)
            split_high(0, 1)
            for k in range(KT):
                for r, n in ((0, 4), (1, 3)):
                    i = 2 * k + r
                    act.wait_ge(s["hT_done"], i + 1)
                    a(h_hi[:, k, r * 512:r * 512 + n * P], [proj[0], proj[1], yt, ob][i // 2][:, i % 2, 0:n * P],
                      ACT.Copy, scale=norm_w[:, k:k + 1]).then_inc(s["h_evac_hi"], 1)
            act.wait_ge(s["dt_proj"], 1)
            a(seqs(conv[:, 0, :]), bank_seqs(proj[0]), ACT.Identity,
              bias=dt_bias[:, 0:1]).then_inc(s["dt_act"], 1)
            act.wait_ge(s["dt_act"], 1)
            a(conv[:, 1, :], conv[:, 0, :], ACT.Abs).then_inc(s["dt_act"], 1)
            act.wait_ge(s["dt_act"], 2)
            a(conv[:, 1, :], conv[:, 1, :], ACT.Exp, scale=-1.0).then_inc(s["dt_act"], 1)
            a(a_exp[:], a_log[:], ACT.Exp).then_inc(s["dt_act"], 1)
            act.wait_ge(s["dt_act"], 4)
            a(conv[:, 1, :], conv[:, 1, :], ACT.Ln, bias=1.0).then_inc(s["dt_act"], 1)
            for i in range(4):
                act.wait_ge(s["cst_done"], i + 1)
                dst = (cs_j if i < 2 else dt_j)[:, 4 * (i % 2):4 * (i % 2) + 4, :]
                a(dst, [yt, ob][i // 2][:, i % 2, :].rearrange("p (q h) -> p q h", q=4),
                  ACT.Copy).then_inc(s["cst_evac"], 1)

            act.wait_ge(s["cs_stored"], 32)

            def first_tap(g, idx, col, m):
                wait(act, s["w_used"], WT, g, idx + 1)
                wait(act, s["silu_done"], 10, g, m - 1)
                a(seqs(conv[:, m % 2, :]), bank_seqs(proj[idx % 2]), ACT.Identity, bias=conv_b[:, bass.ds(col, 1)],
                  scale=conv_w[:, bass.ds(col, 1), TAPS - 1]).then_inc(s["tap0_done"], 1)

            def silu(g, m, dst):
                wait(act, s["conv_tap"], 30, g, 3 * m + 3)
                if m < 2:
                    wait(act, s["cb_done"], 1, g, 0)
                a(real(dst), seqs(conv[:, m % 2, :]), ACT.Silu).then_inc(s["silu_done"], 1)

            def silu_gate(g, c):
                wait(act, s["w_used"], WT, g, 4 + 2 * c)
                wait(act, s["p_done"], CT, g, c - 1)
                a(seqs(gate[:, c % 2, :]), bank_seqs(proj[1]), ACT.Silu).then_inc(s["gate_done"], 1)

            def half_free(g, c):
                if 0 <= c < 4:
                    wait(act, s["outb_done"], TT, g, 0)
                else:
                    wait(act, s["outa_done"], TT, g, TT if c >= 4 else 0)

            def y_high(g, c):
                if not within(g, c):
                    return
                wait(act, s["p_done"], CT, g, c + 1)
                if c % CT == 0:
                    wait(act, s["ss_done"], 1, g, 0)
                    a(sqsum[:], yg[:, c % 2, :], ACT.Square)
                else:
                    wait(act, s["sqsum_done"], 7, g, c - 1 if c > 0 else c)
                    a(sq[:], yg[:, c % 2, :], ACT.Square).then_inc(s["sq_done"], 1)
                half_free(g, c)
                a(y_hi[:, c % 4, :], yg[:, c % 2, :], ACT.Copy).then_inc(s["y_high"], 1)

            def wo_high(g, c):
                if not within(g, c):
                    return
                wait(act, wo_loaded[c % 2], 64, g, 16 * (c // 2 + 1))
                half_free(g, c)
                a(wo_hi[:, c % 4, :], wo_raw[:, c % 2, :], ACT.Copy,
                  scale=gnorm[:, bass.ds(g * CT + c, 1)]).then_inc(s["wo_high"], 1)

            def distance(g, c):
                if not within(g, c):
                    return
                wait(act, s["d_done"], CT, g, c + 1)
                a(decay[:, c % 4, :], decay[:, c % 4, :], ACT.Abs).then_inc(s["abs_done"], 1)

            def exps(g, c0):
                for c in range(c0, c0 + 4):
                    wait(act, s["abs_done"], CT, g, c + 1)
                    a(decay[:, c % 4, :], decay[:, c % 4, :], ACT.Exp, scale=-1.0).then_inc(s["exp_done"], 1)

            for c in range(2):
                distance(0, c)

            def group(g, steps=CT):
                live = has_group(g)
                for st in range(steps):
                    distance(g, st + 2)
                    if live and st % 4 == 1:
                        exps(g, st - 1)
                    if st == 0:
                        y_high(g, -2)
                        wo_high(g, -2)
                    if live:
                        if st == 0:
                            split_high(g, 2)
                            first_tap(g, 0, g * 1 + 64, 0)
                            split_high(g, 3)
                            silu(g, 0, bmat[:])
                            first_tap(g, 1, g * 1 + 72, 1)
                            split_high(g, 4)
                            silu(g, 1, cmat[:])
                        else:
                            split_high(g, 4 + 2 * st)
                    if st:
                        y_high(g, st - 2)
                        wo_high(g, st - 2)
                    if live:
                        first_tap(g, 2 + 2 * st, g * CT + st, 2 + st)
                        split_high(g, 5 + 2 * st)
                        wait(act, s["yres_done"], CT, g, st - 1)
                        silu(g, 2 + st, hid[:, st % 2, :])
                        silu_gate(g, st)
                        if st == 5:
                            for t in range(TT):
                                wait(act, s["outa_done"], TT, g, t + 1)
                                wait(act, s["sum_done"], TT, g, 0)
                                a(part[:, t, :], ob[:, t % 2, :], ACT.Copy).then_inc(s["outa_evac"], 1)
            over_groups(act, group)
            group(GROUPS, 2)

            def transposed_keys(n, u):
                for i in range(0, 24, 2):
                    dt, q, j = i // 6, i % 6 // 3, i % 3
                    wait(act, s["k_tr"], 48, n, 24 * u + i + 1)
                    if i % 6 == 0:
                        wait(act, s["s_mm"], 8, n, 4 * u + dt - 1)
                    a(keysT[:, dt % 2, q, 4 * KP * j:4 * KP * (j + 1)], kt_bank[0][:, 0:4 * KP],
                      ACT.Copy).then_inc(s["kev_act"], 1)

            def router_exp(n, u):
                wait(act, s["lg_done"], 2, n, u + 1)
                a(S["le"], S["lg"], ACT.Exp, bias=S["nlm"], accum_out=S["lsum"]).then_inc(s["le_done"], 1)

            def pairs(n):
                for u in range(2):
                    transposed_keys(n, u)
                    wait(act, s["nmax_done"], 2, n, u + 1)
                    wait(act, s["pT_tr"], 6, n, 3 * u)
                    wait(act, s["z2_done"], 2, n, u)
                    a(probs[:].rearrange("p (c n) -> p c n", c=3), scores, ACT.Exp, bias=S["nmax"],
                      accum_out=S["esum"]).then_inc(s["exps_done"], 1)
                    if pair_exists(n, u - 1):
                        router_exp(n, u - 1)
            over_pairs(act, pairs)
            router_exp(PAIRS // 2, -1)

        @block.vector
        def _(dve):
            v = nc.vector
            dve.wait_ge(s["sqs_done"], TT)
            v.tensor_scalar(ms0[:], ssq0[:], 1.0 / DM, RMS_EPS, ALU.mult, ALU.add).then_inc(s["ms0_set"], 1)
            dve.wait_ge(s["r0_set"], 1)
            for t in range(TT):
                v.tensor_scalar(part[:, t, :], part[:, t, :], r0[:, t:t + 1], None,
                                ALU.mult).then_inc(s["h_scaled"], 1)
            v.memset(hid[:].rearrange("p a n -> p (a n)"), 0.0).then_inc(s["dt_dve"], 1)
            for k in range(KT):
                for r, n in ((0, 4), (1, 3)):
                    i = 2 * k + r
                    dve.wait_ge(s["h_evac_hi"], i + 1)
                    v.scalar_tensor_tensor(out=h_lo[:, k, r * 512:r * 512 + n * P],
                                           in0=[proj[0], proj[1], yt, ob][i // 2][:, i % 2, 0:n * P],
                                           scalar=norm_w[:, k:k + 1],
                                           in1=h_hi[:, k, r * 512:r * 512 + n * P].bitcast(f32),
                                           op0=ALU.mult, op1=ALU.subtract).then_inc(s["h_evac_lo"], 1)
            dve.wait_ge(s["dt_act"], 5)
            dve.wait_ge(s["dt_dve"], 1)
            v.scalar_tensor_tensor(out=real(hid[:, 1, :]), in0=seqs(conv[:, 0, :]), scalar=0.0,
                                   in1=seqs(conv[:, 1, :]), op0=ALU.max, op1=ALU.add).then_inc(s["dt_dve"], 1)
            dve.wait_ge(s["dt_dve"], 2)
            v.tensor_scalar(seqs(conv[:, 0, :]), real(hid[:, 1, :]), a_exp[:, 0:1], -1.0, ALU.mult,
                            ALU.mult).then_inc(s["dt_dve"], 1)
            keep = conv[:, 1, :]
            v.memset(keep, 1.0).then_inc(s["dt_dve"], 1)
            dve.wait_ge(s["dt_dve"], 4)
            v.memset(keep.rearrange("p (b i) -> p b i", i=LEN)[:, :, 0:1], 0.0).then_inc(s["dstep"], 1)
            dve.wait_ge(s["dstep"], 1)
            v.tensor_tensor_scan(sq[:], keep, conv[:, 0, :], 0.0, ALU.mult, ALU.add).then_inc(s["dstep"], 1)
            dve.wait_ge(s["dstep"], 2)
            v.tensor_copy(real(hid[:, 0, :]), seqs(sq[:])).then_inc(s["dt_dve"], 1)
            dve.wait_ge(s["cst_evac"], 4)

            def taps(g, idx, col, m):
                dst, src = seqs(conv[:, m % 2, :]), bank_seqs(proj[idx % 2])
                for sh in range(1, TAPS):
                    if sh == 1:
                        wait(dve, s["tap0_done"], 10, g, m + 1)
                    else:
                        wait(dve, s["conv_tap"], 30, g, 3 * m + sh - 1)
                    v.scalar_tensor_tensor(out=dst[:, :, sh:LEN], in0=src[:, :, 0:LEN - sh],
                                           scalar=conv_w[:, bass.ds(col, 1), TAPS - 1 - sh],
                                           in1=dst[:, :, sh:LEN], op0=ALU.mult,
                                           op1=ALU.add).then_inc(s["conv_tap"], 1)

            def finish_y(g, c):
                if not within(g, c):
                    return
                wait(dve, s["y_done"], CT, g, c + 1)
                wait(dve, s["y_low"], CT, g, c - 1)
                v.scalar_tensor_tensor(out=seqs(yg[:, c % 2, :]), in0=real(hid[:, c % 2, :]),
                                       scalar=skip[:, bass.ds(g * CT + c, 1)], in1=bank_seqs(yt),
                                       op0=ALU.mult, op1=ALU.add).then_inc(s["yres_done"], 1)
                wait(dve, s["gate_done"], CT, g, c + 1)
                wait(dve, s["yres_done"], CT, g, c + 1)
                v.tensor_tensor(yg[:, c % 2, :], yg[:, c % 2, :], gate[:, c % 2, :],
                                ALU.mult).then_inc(s["p_done"], 1)

            def wo_low(g, c):
                if not within(g, c):
                    return
                wait(dve, s["wo_high"], CT, g, c + 1)
                v.scalar_tensor_tensor(out=wo_lo[:, c % 4, :], in0=wo_raw[:, c % 2, :],
                                       scalar=gnorm[:, bass.ds(g * CT + c, 1)],
                                       in1=wo_hi[:, c % 4, :].bitcast(f32), op0=ALU.mult,
                                       op1=ALU.subtract).then_inc(s["wo_low"], 1)

            def scale_hid(g, c):
                if not within(g, c):
                    return
                for r in range(2):
                    wait(dve, s["t_done"], 2 * CT, g, 2 * c + r + 1)
                    v.tensor_tensor(
                        hd_dt[:, 4 * r:4 * r + 4, :].rearrange("p q (h d) -> p q h d", h=2),
                        yt[:, r, :].rearrange("p (q h d) -> p q h d", q=4, h=2),
                        bc(dt_j[:, 4 * r:4 * r + 4, bass.ds(g * 16 + 2 * c, 2)], 3, HD),
                        ALU.mult).then_inc(s["hd_done"], 1)

            def differences(g, c):
                if not within(g, c):
                    return
                wait(dve, cs_loaded[c % 4], 64, g, 32 * (c // 4 + 1))
                t = decay[:, c % 4, :].rearrange("p (h q i) -> p h q i", h=2, i=LEN)
                v.tensor_tensor(t, t, bc(cs_j[:, :, bass.ds(g * 16 + 2 * c, 2)].rearrange("p q h -> p h q"), 3, LEN),
                                ALU.subtract).then_inc(s["d_done"], 1)

            def mix_high(g, c):
                if not within(g, c):
                    return
                wait(dve, s["exp_done"], CT, g, c + 1)
                wait(dve, s["y_done"], CT, g, c)
                wait(dve, s["cbm_done"], 1, g, 1 if c >= 0 else 0)
                v.scalar_tensor_tensor(
                    out=mixw[PAD:P, :, :, LEN:2 * LEN],
                    in0=decay[PAD:P, c % 4, :].rearrange("p (h q i) -> p h q i", h=2, i=LEN), scalar=1.0,
                    in1=bc(cbm[PAD:P, :, :], 1, 2), op0=ALU.mult, op1=ALU.mult).then_inc(s["m_hi_done"], 1)

            def mask_cb(g):
                wait(dve, s["m_lo_done"], CT, g, 0)
                wait(dve, s["m_hi_done"], CT, g, 0)
                wait(dve, s["cb_done"], 1, g, 1)
                v.tensor_tensor(cbm[:], ob[:, 0, 0:PAIRS * LEN].rearrange("p (q i) -> p q i", i=LEN),
                                bc(causal[:], 1, PAIRS), ALU.mult).then_inc(s["cbm_done"], 1)

            def group_squares(g):
                wait(dve, s["ss_done"], 1, g, 0)
                v.tensor_scalar(ms[:], ob[:, 0, 0:TT], 1.0 / (CT * P), RMS_EPS, ALU.mult,
                                ALU.add).then_inc(s["ms_done"], 1)

            def add_output(g, t):
                wait(dve, s["outb_done"], TT, g, t - TT + 1)
                if t == 0:
                    wait(dve, s["outa_evac"], TT, g, 0)
                    wait(dve, s["rg_done"], 1, g, 0)
                v.tensor_tensor(part[:, t, :], ob[:, (t + 1) % 2, :], part[:, t, :],
                                ALU.add).then_inc(s["psum_added"], 1)
                wait(dve, s["psum_added"], TT, g, t - TT + 1)
                v.scalar_tensor_tensor(out=acc[:, t, :], in0=part[:, t, :], scalar=rg[:, t:t + 1],
                                       in1=acc[:, t, :], op0=ALU.mult, op1=ALU.add).then_inc(s["sum_done"], 1)

            dve.wait_ge(s["zeroed"], 1)
            v.tensor_copy(causal[PAD:P, :], causal_hi[PAD:P, :]).then_inc(s["dstep"], 1)
            dve.wait_ge(s["dstep"], 3)
            for c in range(3):
                differences(0, c)

            def group(g, steps=CT):
                live = has_group(g)
                first = isinstance(g, int) and g == 0
                for st in range(steps):
                    finish_y(g, st - 2)
                    mix_high(g, st - 1)
                    wo_low(g, st - 2)
                    if live and st == 0:
                        taps(g, 0, g * 1 + 64, 0)
                        taps(g, 1, g * 1 + 72, 1)
                    scale_hid(g, st - 1)
                    if live:
                        taps(g, 2 + 2 * st, g * CT + st, 2 + st)
                    differences(g, st + 3)
                    if st == 1 and not first:
                        group_squares(g)
                        for t in range(TT):
                            add_output(g, t)
                    if live and st == 0:
                        mask_cb(g)
            over_groups(dve, group)
            group(GROUPS, 2)

            dve.wait_ge(s["xres_loaded"], 16)
            dve.wait_ge(s["sum_done"], GROUPS * TT)
            xres = decay[:].rearrange("p a n -> p (a n)").rearrange("p (t d) -> p t d", t=TT)
            for t in range(TT):
                v.scalar_tensor_tensor(out=acc[:, t, :], in0=xres[:, t, :], scalar=2.0, in1=acc[:, t, :],
                                       op0=ALU.mult, op1=ALU.add).then_inc(s["ln1_step"], 1)
                dve.wait_ge(s["ln1_step"], 3 * t + 1)
                v.bn_stats(stats[:], acc[:, t, :]).then_inc(s["ln1_step"], 1)
                dve.wait_ge(s["ln1_step"], 3 * t + 2)
                v.bn_aggr(mv1[:, t, :], stats[:]).then_inc(s["ln1_step"], 1)
                dve.wait_ge(s["ln1_step"], 3 * t + 3)
            v.tensor_scalar(var1[:], mv1[:, :, 1], LN_EPS, None, ALU.add).then_inc(s["ln1_var"], 1)
            dve.wait_ge(s["ln1_rstd"], 1)
            for t in range(TT):
                v.tensor_scalar(acc[:, t, :], acc[:, t, :], mv1[:, t, 0:1], rstd1[:, t:t + 1],
                                ALU.subtract, ALU.mult).then_inc(s["x1_set"], 1)

            NORM2, ROUTE, NORM3 = 2, 16, 3
            STEPS = 2 * (NORM2 + ROUTE + NORM3)

            def link(ins, n, cell):
                ins.then_inc(s["dstep"], 1)
                cell[0] += 1
                wait(dve, s["dstep"], STEPS, n, cell[0])

            def link_one(ins):
                ins.then_inc(s["stats_set"], 1)
                dve.wait_ge(s["stats_set"], 1)
                dve.sem_inc(s["stats_set"], -1)

            def queries(n, u):
                wait(dve, s["q_tr"], 2, n, u + 1)
                wait(dve, s["s_mm"], 8, n, 4 * u)
                v.tensor_copy(qT[:], misc.rearrange("p (k t) -> p k t", k=KT)).then_inc(s["q_evac"], 1)

            def transposed_keys(n, u, lo, hi):
                for i in range(2 * lo + 1, 2 * hi, 2):
                    dt, q, j = i // 6, i % 6 // 3, i % 3
                    wait(dve, s["k_tr"], 48, n, 24 * u + i + 1)
                    if i % 6 == 1:
                        wait(dve, s["s_mm"], 8, n, 4 * u + dt - 1)
                    v.tensor_copy(keysT[:, dt % 2, q, 4 * KP * j:4 * KP * (j + 1)],
                                  kt_bank[1][:, 0:4 * KP]).then_inc(s["kev_dve"], 1)

            def score_max(n, u):
                wait(dve, s["s_mm"], 8, n, 4 * u + 4)
                wait(dve, s["exps_done"], 2, n, u)
                v.tensor_reduce(S["nmax"], scores, AX.XY, ALU.max, negate=True).then_inc(s["nmax_done"], 1)

            def transposed_probs(n, u):
                for r in range(3):
                    wait(dve, s["pT_tr"], 6, n, 3 * u + r + 1)
                    if r == 0:
                        wait(dve, s["pv_done"], 2, n, u)
                    v.tensor_copy(probsT[0:KP, 4 * r:4 * r + 4, :],
                                  bank[0:KP, r, :].rearrange("p (j t) -> p j t", j=4)).then_inc(s["pT_evac"], 1)

            def norm2_sum(n, u, cell):
                wait(dve, s["exps_done"], 2, n, u + 1)
                link(v.reciprocal(S["rsum"], S["esum"]), n, cell)
                wait(dve, s["pv_done"], 2, n, u + 1)
                v.scalar_tensor_tensor(out=x2[:, u, :], in0=pv, scalar=S["rsum"], in1=x1p[:, u, :],
                                       op0=ALU.mult, op1=ALU.add).then_inc(s["z2_done"], 1)

            def norm2_stats(n, u, cell):
                wait(dve, s["z2_done"], 2, n, u + 1)
                link_one(v.bn_stats(S["st2"], x2[:, u % 2, :]))
                link(v.bn_aggr(S["mv2"], S["st2"]), n, cell)
                v.tensor_scalar(S["var2"], S["mv2"][:, 1:2], LN_EPS, None, ALU.add).then_inc(s["var2_done"], 1)

            def norm2_apply(n, u):
                wait(dve, s["rstd2_done"], 2, n, u + 1)
                v.tensor_scalar(x2[:, u % 2, :], x2[:, u % 2, :], S["mv2"][:, 0:1], S["rstd2"], ALU.subtract,
                                ALU.mult).then_inc(s["x2_done"], 1)

            def x2_transposed(n, u):
                wait(dve, s["x2_tr"], 2, n, u + 1)
                v.tensor_copy(x2T[:], misc.rearrange("p (k t) -> p k t", k=KT)).then_inc(s["x2_evac"], 1)

            def route(n, u, cell):
                wait(dve, s["route_done"], 2, n, u + 1)
                link(v.tensor_copy(S["lg"], misc[:, P:P + EXP]), n, cell)
                v.tensor_reduce(S["nlm"], S["lg"], AX.X, ALU.max, negate=True).then_inc(s["lg_done"], 1)
                wait(dve, s["le_done"], 2, n, u + 1)
                link(v.reciprocal(S["lr"], S["lsum"]), n, cell)
                link(v.tensor_scalar(S["pr"], S["le"], S["lr"], None, ALU.mult), n, cell)
                link(v.tensor_reduce(S["v1"], S["pr"], AX.X, ALU.max), n, cell)
                link(v.scalar_tensor_tensor(out=S["k1"], in0=S["pr"], scalar=S["v1"], in1=order[:],
                                            op0=ALU.is_equal, op1=ALU.mult), n, cell)
                link(v.tensor_reduce(S["km1"], S["k1"], AX.X, ALU.max), n, cell)
                link(v.tensor_scalar(S["oh1"], order[:], S["km1"], None, ALU.is_equal), n, cell)
                link(v.scalar_tensor_tensor(out=S["p2"], in0=S["oh1"], scalar=-4.0, in1=S["pr"], op0=ALU.mult,
                                            op1=ALU.add), n, cell)
                link(v.tensor_reduce(S["v2"], S["p2"], AX.X, ALU.max), n, cell)
                link(v.scalar_tensor_tensor(out=S["k2"], in0=S["p2"], scalar=S["v2"], in1=order[:],
                                            op0=ALU.is_equal, op1=ALU.mult), n, cell)
                link(v.tensor_reduce(S["km2"], S["k2"], AX.X, ALU.max), n, cell)
                link(v.scalar_tensor_tensor(out=S["sel"], in0=order[:], scalar=S["km2"], in1=S["oh1"],
                                            op0=ALU.is_equal, op1=ALU.add), n, cell)
                link(v.tensor_tensor(S["top"], S["sel"], S["pr"], ALU.mult), n, cell)
                link(v.tensor_reduce(S["tsum"], S["top"], AX.X, ALU.add), n, cell)
                link(v.reciprocal(S["tr"], S["tsum"]), n, cell)
                link(v.tensor_scalar(S["wgt"], S["top"], S["tr"], LORA_SCALE, ALU.mult, ALU.mult), n, cell)
                v.tensor_tensor(hw[:].rearrange("p (e r) -> p e r", r=RANK),
                                misc[:, 0:P].rearrange("p (e r) -> p e r", r=RANK), bc(S["wgt"], 2, RANK),
                                ALU.mult).then_inc(s["hw_done"], 1)

            def hw_transposed(n, u):
                wait(dve, s["hw_tr"], 2, n, u + 1)
                v.tensor_copy(hwT[:], misc[:, 0:P]).then_inc(s["hw_evac"], 1)

            def norm3_sum(n, u, cell):
                sl = u % 2
                wait(dve, s["ffn_done"], 2, n, u + 1)
                wait(dve, stored[sl], 32, n, 32 * (u // 2))
                link(v.tensor_tensor(z3[:, sl, :], ffn, x2[:, sl, :], ALU.add), n, cell)

            def norm3_bias(n, u, cell):
                sl = u % 2
                link(v.tensor_tensor(z3[:, sl, :], z3[:, sl, :], bias[:], ALU.add), n, cell)

            def norm3_stats(n, u, cell):
                link_one(v.bn_stats(S["st3"], z3[:, u % 2, :]))
                link(v.bn_aggr(S["mv3"], S["st3"]), n, cell)
                v.tensor_scalar(S["var3"], S["mv3"][:, 1:2], LN_EPS, None, ALU.add).then_inc(s["var3_done"], 1)

            def norm3_apply(n, u):
                sl = u % 2
                wait(dve, s["rstd3_done"], 2, n, u + 1)
                v.tensor_scalar(z3[:, sl, :], z3[:, sl, :], S["mv3"][:, 0:1], S["rstd3"], ALU.subtract,
                                ALU.mult).then_inc(s["out_ready"], 1)

            dve.wait_ge(s["order_set"], 2)
            dve.wait_ge(s["ffn_loaded"], 64)

            def pairs(n):
                cell = [3 if isinstance(n, int) and n == 0 else 3 - 1 - ROUTE - 2 * NORM3]
                for u in range(2):
                    before, before2 = pair_exists(n, u - 1), pair_exists(n, u - 2)
                    queries(n, u)
                    transposed_keys(n, u, 0, 3)
                    if before:
                        norm2_stats(n, u - 1, cell)
                    transposed_keys(n, u, 3, 4)
                    if before:
                        norm2_apply(n, u - 1)
                    transposed_keys(n, u, 4, 5)
                    if before2:
                        norm3_sum(n, u - 2, cell)
                    transposed_keys(n, u, 5, 6)
                    if before2:
                        norm3_bias(n, u - 2, cell)
                    transposed_keys(n, u, 6, 7)
                    if before2:
                        norm3_stats(n, u - 2, cell)
                    transposed_keys(n, u, 7, 8)
                    if before2:
                        norm3_apply(n, u - 2)
                    transposed_keys(n, u, 8, 12)
                    if before:
                        x2_transposed(n, u - 1)
                    score_max(n, u)
                    transposed_probs(n, u)
                    if before:
                        route(n, u - 1, cell)
                        hw_transposed(n, u - 1)
                    norm2_sum(n, u, cell)
            over_pairs(dve, pairs)
            cell = [3 - 1 - ROUTE - 2 * NORM3]
            norm2_stats(PAIRS // 2, -1, cell)
            norm2_apply(PAIRS // 2, -1)
            norm3_sum(PAIRS // 2, -2, cell)
            norm3_bias(PAIRS // 2, -2, cell)
            norm3_stats(PAIRS // 2, -2, cell)
            norm3_apply(PAIRS // 2, -2)
            x2_transposed(PAIRS // 2, -1)
            route(PAIRS // 2, -1, cell)
            hw_transposed(PAIRS // 2, -1)
            norm3_sum(PAIRS // 2, -1, cell)
            norm3_bias(PAIRS // 2, -1, cell)
            norm3_stats(PAIRS // 2, -1, cell)
            norm3_apply(PAIRS // 2, -1)

        @block.tensor
        def _(pe):
            mm, tr = nc.tensor.matmul, nc.tensor.transpose
            pe.wait_ge(s["consts_set"], 1)
            for k in range(KT):
                for r, n in ((0, 4), (1, 3)):
                    i = 2 * k + r
                    for q in range(n):
                        t = 4 * r + q
                        pe.wait_ge(s["h_scaled"], t + 1)
                        last = tr([proj[0], proj[1], yt, ob][i // 2][:, i % 2, q * P:(q + 1) * P],
                                  part[:, t, k * P:(k + 1) * P], ident[:])
                    last.then_inc(s["hT_done"], 1)

            def product(out, hi, lo):
                for k in range(KT):
                    for i, (w, x) in enumerate(((hi, h_hi), (hi, h_lo), (lo, h_hi))):
                        for half in range(2):
                            last = mm(out[:, half, :].rearrange("p (b i) -> p b i", i=PAD)[:, :, 0:LEN], w[:, k * P:(k + 1) * P],
                                      x[:, k, half * HALF:(half + 1) * HALF],
                                      start=(k == 0 and i == 0), stop=(k == KT - 1 and i == 2))
                return last

            pe.wait_ge(s["h_evac_lo"], 8)
            pe.wait_ge(s["dtw_lo"], 1)
            product(proj[0], wo_hi[:, 0, :], wo_lo[:, 0, :]).then_inc(s["dt_proj"], 1)
            pe.wait_ge(s["dt_dve"], 5)
            for i in range(4):
                for q in range(4):
                    pair = 4 * (i % 2) + q
                    last = tr([yt, ob][i // 2][:, i % 2, q * P:(q + 1) * P],
                              hid[:, i // 2, pair * P:(pair + 1) * P], ident[:])
                last.then_inc(s["cst_done"], 1)
            pe.wait_ge(s["cst_evac"], 4)

            def project(g, idx):
                wait(pe, s["w_low"], WT, g, idx + 1)
                product(proj[idx % 2], w_hi[:, idx % 3, :], w_lo[:, idx % 3, :]).then_inc(s["w_used"], 1)

            def transpose_hid(g, c):
                if not within(g, c):
                    return
                wait(pe, s["silu_done"], 10, g, c + 3 if c >= 0 else c + 1)
                wait(pe, s["yres_done"], CT, g, c)
                for r in range(2):
                    for q in range(4):
                        pair = 4 * r + q
                        last = tr(yt[:, r, q * P:(q + 1) * P], hid[:, c % 2, pair * P:(pair + 1) * P], ident[:])
                    last.then_inc(s["t_done"], 1)

            def y_product(g, c):
                if not within(g, c):
                    return
                wait(pe, s["hd_done"], 2 * CT, g, 2 * c + 2)
                wait(pe, s["m_lo_done"], CT, g, c + 1)
                wait(pe, s["m_hi_done"], CT, g, c + 1)
                for pair in range(PAIRS):
                    for h in range(2):
                        place = yt[HD * h:HD * (h + 1), pair // 4, pair % 4 * P:(pair % 4 + 1) * P]
                        last = mm(place.rearrange("p (s i) -> p s i", i=PAD)[:, :, 0:LEN],
                                  hd_dt[:, pair, HD * h:HD * (h + 1)], mixw[:, h, pair, :], start=True, stop=True)
                last.then_inc(s["y_done"], 1)

            def cb_product(g):
                wait(pe, s["silu_done"], 10, g, 2)
                wait(pe, s["outa_evac"], TT, g, 0)
                for b in range(SEQS):
                    last = mm(ob[PAD * (b % 2):PAD * (b % 2 + 1), 0, b // 2 * LEN:(b // 2 + 1) * LEN],
                              bmat[:, b * PAD:(b + 1) * PAD], cmat[:, b * PAD:b * PAD + LEN], start=True, stop=True)
                last.then_inc(s["cb_done"], 1)

            def out_product(t, b):
                for c in range(4):
                    tok = slice(t * P, (t + 1) * P)
                    for i, (y, w) in enumerate(((y_hi, wo_hi), (y_hi, wo_lo), (y_lo, wo_hi))):
                        last = mm(ob[:, b, :], y[:, c, tok], w[:, c, :], start=(c == 0 and i == 0),
                                  stop=(c == 3 and i == 2))
                return last

            def second_half(g):
                wait(pe, s["sqsum_done"], 7, g, 0)
                if has_group(g):
                    wait(pe, s["cbm_done"], 1, g, 1)
                else:
                    wait(pe, s["outa_evac"], TT, g, 0)
                for t in range(TT):
                    last = mm(ob[:, 0, t:t + 1], sqsum[:, t * P:(t + 1) * P], ones[:], start=True, stop=True)
                last.then_inc(s["ss_done"], 1)
                wait(pe, s["y_low"], CT, g, 0)
                wait(pe, s["wo_low"], CT, g, 0)
                for t in range(TT):
                    if t == 1:
                        wait(pe, s["rg_done"], 1, g, 0)
                    elif t > 1:
                        wait(pe, s["psum_added"], TT, g, t - 1 - TT)
                    last = out_product(t, (t + 1) % 2)
                    last.then_inc(s["outb_done"], 1)

            def first_half(g):
                wait(pe, s["y_low"], CT, g, 4)
                wait(pe, s["wo_low"], CT, g, 4)
                wait(pe, s["psum_added"], TT, g, 0)
                wait(pe, s["cbm_done"], 1, g, 1)
                for t in range(TT):
                    if t > 1:
                        wait(pe, s["outa_evac"], TT, g, t - 1)
                    out_product(t, t % 2).then_inc(s["outa_done"], 1)

            def group(g, steps=CT):
                live = has_group(g)
                for st in range(steps):
                    if live and st == 0:
                        wait(pe, s["conv_tap"], 30, g, 0)
                        project(g, 0)
                        wait(pe, s["gate_done"], CT, g, 0)
                        project(g, 1)
                    if live:
                        wait(pe, s["conv_tap"], 30, g, 3 * st + 6 if st else 3)
                        project(g, 2 + 2 * st)
                    transpose_hid(g, st - 1)
                    if live:
                        if st:
                            wait(pe, s["gate_done"], CT, g, st)
                        else:
                            wait(pe, s["conv_tap"], 30, g, 6)
                        project(g, 3 + 2 * st)
                    if live and st == 0:
                        cb_product(g)
                    if st == 1 and not (isinstance(g, int) and g == 0):
                        second_half(g)
                    if live and st == 5:
                        first_half(g)
                    y_product(g, st - 1)
            over_groups(pe, group)
            group(GROUPS, 2)

            def to_channels(src, done):
                for k in range(KT):
                    last = tr(misc[:, k * P:(k + 1) * P], src[:, k * P:(k + 1) * P], ident[:])
                last.then_inc(done, 1)

            def transpose_keys(n, u, dt, part_of):
                for i in range(6 * dt + 2 * part_of, 6 * dt + 2 * part_of + 2):
                    q, j0 = i % 6 // 3, 4 * (i % 3)
                    if i % 2:
                        wait(pe, s["kev_dve"], 24, n, 12 * u + i // 2)
                    else:
                        wait(pe, s["kev_act"], 24, n, 12 * u + i // 2)
                    for j in range(4):
                        last = tr(kt_bank[i % 2][:, j * KP:(j + 1) * KP],
                                  keys[0:KP, u, q, j0 + j, dt * P:(dt + 1) * P], ident[0:KP, 0:KP])
                    last.then_inc(s["k_tr"], 1)

            def score(n, u, dt, c):
                if c == 0:
                    wait(pe, s["kev_act"], 24, n, 12 * u + 3 * dt + 3)
                    wait(pe, s["kev_dve"], 24, n, 12 * u + 3 * dt + 3)
                    if dt == 0:
                        wait(pe, s["q_evac"], 2, n, u + 1)
                        wait(pe, s["exps_done"], 2, n, u)
                        wait(pe, s["pT_evac"], 6, n, 3 * u)
                for q in range(2):
                    last = mm(scores[PAD * q:PAD * (q + 1), c, :], qT[:, dt, PAD * q:PAD * (q + 1)],
                              keysT[:, dt % 2, q, c * 500:(c + 1) * 500], start=(dt == 0), stop=(dt == KT - 1))
                if c == 2:
                    last.then_inc(s["s_mm"], 1)

            def transpose_x2(n, u):
                if not (isinstance(n, int) and n == PAIRS // 2):
                    wait(pe, s["q_evac"], 2, n, u + 2)
                wait(pe, s["x2_done"], 2, n, u + 1)
                to_channels(x2[:, u % 2, :], s["x2_tr"])

            def feed_forward(n, u):
                wait(pe, s["x2_evac"], 2, n, u + 1)
                for k in range(KT):
                    last = mm(misc[:, 0:P + EXP], x2T[:, k, :], waT[:, k, :], start=(k == 0), stop=(k == KT - 1))
                last.then_inc(s["route_done"], 1)
                wait(pe, s["rstd3_done"], 2, n, u)
                for k in range(KT):
                    mm(ffn, x2T[:, k, :], wbT[:, k, :], start=(k == 0), stop=False)

            def transpose_hw(n, u):
                wait(pe, s["hw_done"], 2, n, u + 1)
                tr(misc[:, 0:P], hw[:], ident[:]).then_inc(s["hw_tr"], 1)

            def lora(n, u):
                wait(pe, s["hw_evac"], 2, n, u + 1)
                mm(ffn, hwT[:], wlb[:], start=False, stop=True).then_inc(s["ffn_done"], 1)

            def transpose_probs(n, u):
                wait(pe, s["exps_done"], 2, n, u + 1)
                for r in range(3):
                    for j in range(4):
                        key = (4 * r + j) * KP
                        last = tr(bank[0:KP, r, j * P:(j + 1) * P], probs[:, key:key + KP], ident[:])
                    last.then_inc(s["pT_tr"], 1)

            def values(n, u, r):
                if r == 0:
                    wait(pe, s["z2_done"], 2, n, u)
                wait(pe, s["pT_evac"], 6, n, 3 * u + r + 1)
                for j in range(4 * r, 4 * r + 4):
                    for q in range(2):
                        last = mm(pv[PAD * q:PAD * (q + 1), :], probsT[0:KP, j, PAD * q:PAD * (q + 1)],
                                  keys[0:KP, u, q, j, :], start=(j == 0), stop=(j == KJ - 1))
                if r == 2:
                    last.then_inc(s["pv_done"], 1)

            def pairs(n):
                for u in range(2):
                    before = pair_exists(n, u - 1)
                    wait(pe, x1_loaded[u], 32, n, 32)
                    wait(pe, s["hw_evac"], 2, n, u - 1)
                    to_channels(x1p[:, u, :], s["q_tr"])
                    wait(pe, keys_loaded[u], 64, n, 64)
                    for c in range(3):
                        transpose_keys(n, u, 0, c)
                    for dt in range(1, KT):
                        for c in range(3):
                            transpose_keys(n, u, dt, c)
                            score(n, u, dt - 1, c)
                    if before:
                        transpose_x2(n, u - 1)
                    for c in range(3):
                        score(n, u, KT - 1, c)
                    if before:
                        feed_forward(n, u - 1)
                    transpose_probs(n, u)
                    values(n, u, 0)
                    values(n, u, 1)
                    if before:
                        transpose_hw(n, u - 1)
                    values(n, u, 2)
                    if before:
                        lora(n, u - 1)
            over_pairs(pe, pairs)
            transpose_x2(PAIRS // 2, -1)
            feed_forward(PAIRS // 2, -1)
            transpose_hw(PAIRS // 2, -1)
            lora(PAIRS // 2, -1)


def layouts(inputs):
    import numpy as np

    def flat(name):
        return np.asarray(inputs[name])

    inner = HEADS * HD
    w = flat("L0_attn_in_proj_w")
    tiles = w[:2 * inner + 2 * GROUPS * P].reshape(-1, P, KT, P)
    gate, hid = tiles[:64], tiles[64:128]
    b, c = tiles[128:128 + GROUPS], tiles[128 + GROUPS:]
    order = []
    for g in range(GROUPS):
        order += [b[g], c[g]]
        for t in range(CT):
            order += [hid[g * CT + t], gate[g * CT + t]]
    w_in = np.stack(order).transpose(0, 3, 2, 1).reshape(GROUPS * WT, P, KT * P)
    w_dt = w[-HEADS:].reshape(HEADS, KT, P).transpose(2, 1, 0).reshape(P, KT * HEADS)
    w_base = flat("L0_ffn_W_base").reshape(DM, KT, P).transpose(2, 1, 0).reshape(P, KT * DM)
    a_rows = flat("L0_ffn_lora_A").reshape(EXP * RANK, DM)
    w_a = np.concatenate([a_rows, flat("L0_ffn_W_router")]).reshape(P + EXP, KT, P).transpose(2, 1, 0)
    return {
        "x": flat("x").reshape(TOK, DM),
        "context": flat("ctx_4096").reshape(SEQS, KP, KJ * DM),
        "w_in": w_in,
        "w_dt": w_dt,
        "w_out": flat("L0_attn_out_proj_w").T.reshape(GROUPS * CT, P, DM),
        "norm_w": flat("L0_attn_norm_w").reshape(KT, P).T,
        "conv_w": flat("L0_attn_conv_w").reshape(80, P, TAPS).transpose(1, 0, 2).reshape(P, 80 * TAPS),
        "conv_b": flat("L0_attn_conv_b").reshape(80, P).T,
        "dt_bias": flat("L0_attn_dt_bias").reshape(HEADS, 1),
        "a_log": flat("L0_attn_A_log").reshape(HEADS, 1),
        "skip": flat("L0_attn_Dp").reshape(GROUPS * CT, 2).T,
        "gnorm": flat("L0_attn_gnorm_w").reshape(GROUPS * CT, P).T,
        "w_base": w_base,
        "b_base": flat("L0_ffn_b_base").reshape(1, DM),
        "w_a": w_a.reshape(P, KT * (P + EXP)),
        "w_b": flat("L0_ffn_lora_B").transpose(0, 2, 1).reshape(EXP * RANK, DM),
    }


def kernel(**inputs):
    import numpy as np
    import concourse.bacc as bacc
    from concourse import mybir as my
    from concourse.bass_utils import run_bass_kernel_spmd

    nc = bacc.Bacc("TRN2", target_bir_lowering=False, num_devices=1)
    arrays, access = {}, {}
    for name, value in layouts(inputs).items():
        value = np.ascontiguousarray(value)
        arrays[f"in_{name}"] = value
        access[name] = nc.dram_tensor(f"in_{name}", value.shape, my.dt.from_np(value.dtype), kind="ExternalInput").ap()
    access["out"] = nc.dram_tensor("out", (TOK, DM), my.dt.float32, kind="ExternalOutput").ap()
    layer_kernel(nc, access)
    result = run_bass_kernel_spmd(nc, [arrays], core_ids=[0])
    return result.results[0]["out"].reshape(SEQS, LEN, DM)
```

```python
import concourse.bass as bass
from concourse import mybir
from contextlib import ExitStack

f32 = mybir.dt.float32
f32r = mybir.dt.float32r
ALU = mybir.AluOpType
ACT = mybir.ActivationFunctionType
AX = mybir.AxisListType

P = 128
SEQS, LEN, DM = 16, 56, 512
TOK = SEQS * LEN
PAD = 64
PAIRS = SEQS // 2
HALF = TOK // 2
KT = DM // P
TT = TOK // P
GROUPS, HEADS, HD = 8, 128, 64
CT = 8
WT = 2 + 2 * CT
CONVS = GROUPS * CT + 2 * GROUPS
TAPS = 4
KEYS = 1500
KJ, KP = 12, 125
EXP, RANK = 8, 16
RMS_EPS = 1e-5
LN_EPS = 1e-5
LORA_SCALE = 2.0
SUB = 32


def bc(ap, axis, n):
    v = ap.unsqueeze(axis)
    shape = list(v.shape)
    shape[axis] = n
    return v.broadcast_to(shape)


def layer_kernel(nc, A):
    ctx = ExitStack()
    with ctx:
        def sb(name, shape, dt=f32, stack=ctx):
            return stack.enter_context(nc.sbuf_tensor(name, shape, dt))

        def pb(name, shape):
            return ctx.enter_context(nc.psum_tensor(name, shape, f32))

        def sem(name):
            return ctx.enter_context(nc.semaphore(name))

        acc = sb("acc", [P, TT, DM])
        ident = sb("ident", [P, P])
        ones = sb("ones", [P, SUB])
        epsc = sb("epsc", [P, TT])
        stats = sb("stats", [P, 6])
        mv1 = sb("mv1", [P, TT, 2])
        var1 = sb("var1", [P, TT])
        nmean1 = sb("nmean1", [P, TT])
        rstd1 = sb("rstd1", [P, TT])
        shift1 = sb("shift1", [P, TT])
        order = sb("order", [P, EXP])

        mix = ExitStack()
        h_hi = sb("h_hi", [P, KT, TOK], f32r, mix)
        h_lo = sb("h_lo", [P, KT, TOK], f32r, mix)
        w_raw = sb("w_raw", [P, 3, KT * P], f32, mix)
        w_hi = sb("w_hi", [P, 3, KT * P], f32r, mix)
        w_lo = sb("w_lo", [P, 3, KT * P], f32r, mix)
        bmat = sb("bmat", [P, SEQS * PAD], f32, mix)
        cmat = sb("cmat", [P, SEQS * PAD], f32, mix)
        conv = sb("conv", [P, 2, TOK], f32, mix)
        hid = sb("hid", [P, 2, SEQS * PAD], f32, mix)
        decay = sb("decay", [P, 4, TOK], f32, mix)
        mixw = sb("mixw", [P, 2, PAIRS, 2 * LEN], f32, mix)
        hd_dt = sb("hd_dt", [P, PAIRS, P], f32, mix)
        gate = sb("gate", [P, 2, TOK], f32, mix)
        cbm = sb("cbm", [P, PAIRS, LEN], f32, mix)
        yg = sb("yg", [P, 2, TOK], f32, mix)
        sq = sb("sq", [P, TOK], f32, mix)
        sqsum = sb("sqsum", [P, TOK], f32, mix)
        wo_raw = sb("wo_raw", [P, 2, DM], f32, mix)
        cs_j = sb("cs_j", [P, PAIRS, HEADS], f32, mix)
        dt_j = sb("dt_j", [P, PAIRS, HEADS], f32, mix)
        conv_w = sb("conv_w", [P, CONVS, TAPS], f32, mix)
        conv_b = sb("conv_b", [P, CONVS], f32, mix)
        skip = sb("skip", [P, GROUPS * CT], f32, mix)
        causal = sb("causal", [P, LEN], f32, mix)
        causal_hi = sb("causal_hi", [P, LEN], f32, mix)
        wo_hi = sb("wo_hi", [P, 4, DM], f32r, mix)
        wo_lo = sb("wo_lo", [P, 4, DM], f32r, mix)
        y_hi = sb("y_hi", [P, 4, TOK], f32r, mix)
        y_lo = sb("y_lo", [P, 4, TOK], f32r, mix)
        part = sb("part", [P, TT, DM], f32, mix)
        gnorm = sb("gnorm", [P, GROUPS * CT], f32, mix)
        norm_w = sb("norm_w", [P, KT], f32, mix)
        dt_bias = sb("dt_bias", [P, 1], f32, mix)
        a_log = sb("a_log", [P, 1], f32, mix)
        a_exp = sb("a_exp", [P, 1], f32, mix)
        ssq0 = sb("ssq0", [P, TT], f32, mix)
        ms0 = sb("ms0", [P, TT], f32, mix)
        r0 = sb("r0", [P, TT], f32, mix)
        ms = sb("ms", [P, TT], f32, mix)
        rg = sb("rg", [P, TT], f32, mix)
        own = sb("own", [P, SUB], f32, mix)
        picked = sb("picked", [P, TT, SUB], f32, mix)
        ssq = sb("ssq", [P, TT], f32, mix)
        spare = part[:].rearrange("p t d -> p (t d)")
        cs_all, dt_all = spare[:, 0:SEQS * PAD], spare[:, SEQS * PAD:2 * SEQS * PAD]
        mix.close()

        att = ExitStack()
        keys = sb("keys", [P, 2, 2, KJ, DM], f32, att)
        keysT = sb("keysT", [P, 2, 2, KEYS], f32, att)
        x1p = sb("x1p", [P, 2, DM], f32, att)
        qT = sb("qT", [P, KT, P], f32, att)
        probs = sb("probs", [P, KEYS], f32, att)
        probsT = sb("probsT", [P, KJ, P], f32, att)
        x2 = sb("x2", [P, 2, DM], f32, att)
        x2T = sb("x2T", [P, KT, P], f32, att)
        wbT = sb("wbT", [P, KT, DM], f32, att)
        waT = sb("waT", [P, KT, P + EXP], f32, att)
        wlb = sb("wlb", [P, DM], f32, att)
        bias = sb("bias", [P, DM], f32, att)
        z3 = sb("z3", [P, 2, DM], f32, att)
        hw = sb("hw", [P, P], f32, att)
        hwT = sb("hwT", [P, P], f32, att)
        smalls = {n: sb("s_" + n, [P, k], f32, att) for n, k in dict(
            nmax=1, esum=1, rsum=1, mv2=2, var2=1, rstd2=1, mv3=2, var3=1, rstd3=1,
            lg=8, nlm=1, le=8, lsum=1, lr=1, pr=8, v1=1, k1=8, km1=1, oh1=8, p2=8, v2=1, k2=8, km2=1,
            sel=8, top=8, tsum=1, tr=1, wgt=8, st2=6, st3=6).items()}
        S = {k: v[:] for k, v in smalls.items()}
        att.close()

        bank = pb("bank", [P, 8, 512])
        proj = [bank[:, 0:2, :], bank[:, 2:4, :]]
        yt = bank[:, 4:6, :]
        ob = bank[:, 6:8, :]
        scores = bank[:, 0:3, 0:KEYS // 3]
        kt_bank = [bank[:, 3, :], bank[:, 4, :]]
        pv = bank[:, 5, :]
        ffn = bank[:, 6, :]
        misc = bank[:, 7, :]

        cs_dram = nc.dram_tensor("cs_scratch", (2, HEADS, PAIRS, LEN), f32).ap()
        x1_dram = nc.dram_tensor("x1_scratch", (TOK, DM), f32).ap()

        names = """params_loaded dtw_loaded consts_set pool_step sqs_done ms0_set r0_set h_scaled
            hT_done h_evac_hi h_evac_lo dtw_hi dtw_lo dt_proj dt_act dt_dve cs_stored cst_done cst_evac
            w_high w_low w_used tap0_done conv_tap silu_done gate_done t_done hd_done y_done yres_done
            p_done y_high y_low sq_done sqsum_done d_done abs_done exp_done m_lo_done m_hi_done cb_done cbm_done
            ss_done ss_picked ss_summed ms_done rg_done outa_done outa_evac outb_done psum_added sum_done
            wo_high wo_low zeroed
            residual_loaded residual_set ln1_step ln1_pool ln1_var ln1_rstd x1_set x1_stored ffn_loaded x1p_zero
            q_tr q_evac k_tr kev_act kev_dve s_mm nmax_done exps_done pT_tr pT_evac pv_done
            z2_done var2_done rstd2_done x2_done x2_tr x2_evac route_done lg_done le_done
            stats_set hw_done hw_tr hw_evac ffn_done var3_done rstd3_done out_ready dstep""".split()
        s = {n: sem(n) for n in names}
        w_loaded = [sem(f"w_loaded{i}") for i in range(3)]
        wo_loaded = [sem(f"wo_loaded{i}") for i in range(2)]
        cs_loaded = [sem(f"cs_loaded{i}") for i in range(4)]
        keys_loaded = [sem(f"keys_loaded{i}") for i in range(2)]
        x_loaded = [sem(f"x_loaded{i}") for i in range(2)]
        x1_loaded = [sem(f"x1_loaded{i}") for i in range(2)]
        stored = [sem(f"stored{i}") for i in range(2)]

        def wait(eng, semaphore, per, g, k):
            if isinstance(g, int):
                if per * g + k > 0:
                    eng.wait_ge(semaphore, per * g + k)
            else:
                eng.wait_ge(semaphore, g * per + k)

        def within(g, c):
            return not isinstance(g, int) or 0 <= g * CT + c < GROUPS * CT

        def has_group(g):
            return not isinstance(g, int) or g < GROUPS

        def w_exists(g, idx):
            return not isinstance(g, int) or g * WT + idx < GROUPS * WT

        def seqs(ap):
            return ap.rearrange("p (b i) -> p b i", b=SEQS)

        def bank_seqs(t):
            return t.rearrange("p h (b i) -> p (h b) i", i=PAD)[:, :, 0:LEN]

        def real(ap):
            return ap.rearrange("p (b i) -> p b i", b=SEQS)[:, :, 0:LEN]

        block = ctx.enter_context(nc.Block())

        def over_groups(eng, body):
            body(0)
            with eng.Fori(1, GROUPS - 1) as g:
                body(g)
            body(GROUPS - 1)

        def over_pairs(eng, body):
            body(0)
            body(1)
            with eng.Fori(2, PAIRS // 2) as n:
                body(n)

        def pair_exists(n, u):
            return not isinstance(n, int) or 2 * n + u >= 0

        @block.sync
        def _(sp):
            x = A["x"].rearrange("(t p) d -> p t d", p=P)
            sp.dma_start(part[:, 0:4, :], x[:, 0:4, :]).then_inc(x_loaded[0], 16)
            sp.dma_start(part[:, 4:TT, :], x[:, 4:TT, :]).then_inc(x_loaded[1], 16)
            sp.dma_start(wo_raw[:, 0, :], A["w_dt"]).then_inc(s["dtw_loaded"], 16)
            for dst, src in ((norm_w[:], A["norm_w"]), (dt_bias[:], A["dt_bias"]), (a_log[:], A["a_log"]),
                             (conv_w[:], A["conv_w"].rearrange("p (t k) -> p t k", k=TAPS)),
                             (conv_b[:], A["conv_b"]), (gnorm[:], A["gnorm"]),
                             (skip[0:HD, :], A["skip"][0:1, :].broadcast_to([HD, GROUPS * CT])),
                             (skip[HD:P, :], A["skip"][1:2, :].broadcast_to([HD, GROUPS * CT]))):
                sp.dma_start(dst, src).then_inc(s["params_loaded"], 16)

            def load_w(g, idx):
                if not w_exists(g, idx):
                    return
                wait(sp, s["w_low"], WT, g, idx - 2)
                sp.dma_start(w_raw[:, idx % 3, :], A["w_in"][g * WT + idx, :, :]
                             ).then_inc(w_loaded[idx % 3], 16)

            def load_wo(g, c):
                if not within(g, c):
                    return
                wait(sp, s["wo_low"], CT, g, c - 1)
                if isinstance(g, int) and g == 0 and c == 0:
                    sp.wait_ge(s["dtw_lo"], 1)
                sp.dma_start(wo_raw[:, c % 2, :], A["w_out"][g * CT + c, :, :]).then_inc(wo_loaded[c % 2], 16)

            def load_cs(g, c):
                if not within(g, c):
                    return
                wait(sp, s["m_lo_done"], CT, g, c - 3)
                wait(sp, s["m_hi_done"], CT, g, c - 3)
                for half in range(2):
                    src = cs_dram[half, bass.ds(g * 16 + 2 * c, 2), :, :].rearrange("h p i -> (h p i)")
                    sp.dma_start(decay[PAD * half:PAD * half + LEN, c % 4, :],
                                 src.unsqueeze(0).broadcast_to([LEN, TOK])).then_inc(cs_loaded[c % 4], 16)

            for idx in range(2):
                load_w(0, idx)
            sp.dma_start(acc[:], x).then_inc(s["residual_loaded"], 16)
            for idx in range(2, 6):
                load_w(0, idx)
            sp.wait_ge(s["dt_dve"], 6)
            for half in range(2):
                sp.dma_start(cs_dram[half].rearrange("h p i -> h p i"),
                             cs_all.rearrange("h (p two i) -> h p two i", two=2, i=PAD)[:, :, half, 0:LEN]
                             ).then_inc(s["cs_stored"], 16)
            sp.wait_ge(s["cs_stored"], 32)
            sp.wait_ge(s["zeroed"], 1)
            for c in range(3):
                load_cs(0, c)

            def group(g):
                for st in range(CT):
                    if st == 0 and not (isinstance(g, int) and g == 0):
                        load_w(g, 4)
                        load_w(g, 5)
                    load_cs(g, st + 3)
                    load_w(g, 6 + 2 * st)
                    load_w(g, 7 + 2 * st)
                    load_wo(g, st)
            over_groups(sp, group)

            def load_keys(n, u):
                for q in range(2):
                    for lo, hi in ((0, 112), (112, KP)):
                        sp.dma_start(keys[lo:hi, u, q].rearrange("p j d -> p (j d)"),
                                     A["context"][n * 4 + 2 * u + q, lo:hi, :]).then_inc(keys_loaded[u], 16)

            def load_x1(n, u):
                for q in range(2):
                    sp.dma_start(x1p[PAD * q:PAD * q + LEN, u, :],
                                 x1_dram[bass.ds(n * 4 * LEN + (2 * u + q) * LEN, LEN), :]).then_inc(x1_loaded[u], 16)

            def store(n, u):
                wait(sp, s["out_ready"], 2, n, u + 1)
                for q in range(2):
                    sp.dma_start(A["out"][bass.ds(n * 4 * LEN + (2 * u + q) * LEN, LEN), :],
                                 z3[PAD * q:PAD * q + LEN, u % 2, :]).then_inc(stored[u % 2], 16)

            sp.wait_ge(s["w_used"], GROUPS * WT)
            sp.wait_ge(s["cb_done"], GROUPS)
            load_keys(0, 0)
            sp.wait_ge(s["p_done"], GROUPS * CT)
            load_keys(0, 1)
            sp.wait_ge(s["x1_set"], 1)
            sp.wait_ge(s["x1p_zero"], 1)
            for q in range(2):
                sp.dma_start(x1p[PAD * q:PAD * q + LEN, 0, :], acc[LEN * q:LEN * (q + 1), 0, :]
                             ).then_inc(x1_loaded[0], 16)
            for t in range(TT):
                sp.wait_ge(s["x1_set"], t + 1)
                sp.dma_start(x1_dram[t * P:(t + 1) * P, :], acc[:, t, :]).then_inc(s["x1_stored"], 16)
            sp.wait_ge(s["outb_done"], GROUPS * TT)
            sp.wait_ge(s["sum_done"], GROUPS * TT)
            for dst, src in ((wbT[:], A["w_base"].rearrange("p (k n) -> p k n", k=KT)),
                             (waT[:], A["w_a"].rearrange("p (k n) -> p k n", k=KT)),
                             (wlb[:], A["w_b"]),
                             (bias[:], A["b_base"].broadcast_to([P, DM]))):
                sp.dma_start(dst, src).then_inc(s["ffn_loaded"], 16)
            sp.wait_ge(s["x1_stored"], 16 * TT)
            load_x1(0, 1)

            def pairs(n, more=True):
                for u in range(2):
                    if pair_exists(n, u - 2):
                        store(n, u - 2)
                    if more:
                        wait(sp, s["pv_done"], 2, n, u + 1)
                        load_keys(n + 1, u)
                        wait(sp, s["z2_done"], 2, n, u + 1)
                        load_x1(n + 1, u)
            pairs(0)
            with sp.Fori(1, PAIRS // 2 - 1) as n:
                pairs(n)
            pairs(PAIRS // 2 - 1, more=False)
            store(PAIRS // 2, -2)
            store(PAIRS // 2, -1)
            for i in range(2):
                sp.wait_ge(stored[i], 32 * PAIRS // 2)

        @block.gpsimd
        def _(pool):
            g_ = nc.gpsimd
            g_.memset(ones[:], 1.0)
            g_.memset(epsc[:], -0.5)
            g_.memset(ident[:], 0.0).then_inc(s["pool_step"], 1)
            g_.memset(causal[:], 1.0)
            g_.memset(causal_hi[:], 1.0).then_inc(s["pool_step"], 1)
            pool.wait_ge(s["pool_step"], 2)
            g_.affine_select(out=ident[:], in_=ident[:], compare_op=ALU.not_equal, fill=1.0, base=0,
                             pattern=[[-1, P]], channel_multiplier=1)
            for mask, base in ((causal, 0), (causal_hi, PAD)):
                last = g_.affine_select(out=mask[:], in_=mask[:], compare_op=ALU.is_ge, fill=0.0, base=base,
                                        pattern=[[1, LEN]], channel_multiplier=-1)
            last.then_inc(s["consts_set"], 1)
            g_.memset(decay[:].rearrange("p a n -> p (a n)"), 0.0)
            g_.memset(mixw[:].rearrange("p a b n -> p (a b n)"), 0.0)
            g_.memset(bmat[:], 0.0)
            for e in range(EXP):
                g_.memset(order[:, e:e + 1], float(EXP - e))
            g_.memset(cmat[:], 0.0).then_inc(s["zeroed"], 1)
            for i, (lo, hi) in enumerate(((0, 4), (4, TT))):
                pool.wait_ge(s["ms0_set"], i + 1)
                g_.tensor_tensor(r0[:, lo:hi], ms0[:, lo:hi], epsc[:, lo:hi], ALU.pow).then_inc(s["r0_set"], 1)

            def split_low(g, idx):
                if not w_exists(g, idx):
                    return
                wait(pool, s["w_high"], WT, g, idx + 1)
                wait(pool, s["w_used"], WT, g, idx - 2)
                slot = idx % 3
                g_.tensor_tensor(w_lo[:, slot, :], w_raw[:, slot, :], w_hi[:, slot, :].bitcast(f32),
                                 ALU.subtract).then_inc(s["w_low"], 1)

            pool.wait_ge(s["dtw_hi"], 1)
            g_.tensor_tensor(wo_lo[:, 0, :], wo_raw[:, 0, :], wo_hi[:, 0, :].bitcast(f32),
                             ALU.subtract).then_inc(s["dtw_lo"], 1)
            split_low(0, 0)
            split_low(0, 1)
            pool.wait_ge(s["residual_loaded"], 16)
            g_.tensor_tensor(acc[:], acc[:], acc[:], ALU.add).then_inc(s["residual_set"], 1)

            def y_low(g, c):
                if not within(g, c):
                    return
                wait(pool, s["y_high"], CT, g, c + 1)
                g_.tensor_tensor(y_lo[:, c % 4, :], yg[:, c % 2, :], y_hi[:, c % 4, :].bitcast(f32),
                                 ALU.subtract).then_inc(s["y_low"], 1)

            def add_squares(g, c):
                if not within(g, c) or c % CT == 0:
                    return
                wait(pool, s["sq_done"], CT, g, c + 1)
                g_.tensor_tensor(out=sqsum[:], in0=sq[:], in1=sqsum[:], op=ALU.add).then_inc(s["sqsum_done"], 1)

            def mix_low(g, c):
                if not within(g, c):
                    return
                wait(pool, s["exp_done"], CT, g, c + 1)
                wait(pool, s["y_done"], CT, g, c)
                wait(pool, s["cbm_done"], 1, g, 1 if c >= 0 else 0)
                g_.tensor_tensor(
                    out=mixw[0:PAD, :, :, 0:LEN],
                    in0=decay[0:PAD, c % 4, :].rearrange("p (h q i) -> p h q i", h=2, i=LEN),
                    in1=bc(cbm[0:PAD, :, :], 1, 2), op=ALU.mult).then_inc(s["m_lo_done"], 1)

            def group_rms(g):
                wait(pool, s["ms_done"], 1, g, 0)
                g_.tensor_tensor(rg[:], ms[:], epsc[:], ALU.pow).then_inc(s["rg_done"], 1)

            def group(g, steps=CT):
                for st in range(steps):
                    mix_low(g, st - 1)
                    if st == 0:
                        split_low(g, 2)
                    y_low(g, st - 2)
                    if st == 0:
                        split_low(g, 3)
                    split_low(g, 4 + 2 * st)
                    add_squares(g, st - 2)
                    split_low(g, 5 + 2 * st)
                    if st == 1 and not (isinstance(g, int) and g == 0):
                        group_rms(g)
            over_groups(pool, group)
            group(GROUPS, 2)

            for t in range(TT):
                pool.wait_ge(s["ln1_var"], 2 * t + 2)
                g_.tensor_tensor(rstd1[:, t:t + 1], var1[:, t:t + 1], epsc[:, 0:1], ALU.pow).then_inc(s["ln1_pool"], 1)
                pool.wait_ge(s["ln1_pool"], t + 1)
                g_.tensor_tensor(shift1[:, t:t + 1], nmean1[:, t:t + 1], rstd1[:, t:t + 1],
                                 ALU.mult).then_inc(s["ln1_rstd"], 1)
                if t == 0:
                    pool.wait_ge(s["wo_low"], GROUPS * CT)
                    g_.memset(x1p[:].rearrange("p a d -> p (a d)"), 0.0).then_inc(s["x1p_zero"], 1)

            def rstd2(n, u):
                if not pair_exists(n, u):
                    return
                wait(pool, s["var2_done"], 2, n, u + 1)
                g_.tensor_tensor(S["rstd2"], S["var2"], epsc[:, 0:1], ALU.pow).then_inc(s["rstd2_done"], 1)

            def rstd3(n, u):
                if not pair_exists(n, u):
                    return
                wait(pool, s["var3_done"], 2, n, u + 1)
                g_.tensor_tensor(S["rstd3"], S["var3"], epsc[:, 0:1], ALU.pow).then_inc(s["rstd3_done"], 1)

            def pairs(n):
                for u in range(2):
                    rstd2(n, u - 1)
                    rstd3(n, u - 2)
            over_pairs(pool, pairs)
            rstd2(PAIRS // 2, -1)
            rstd3(PAIRS // 2, -2)
            rstd3(PAIRS // 2, -1)

        @block.scalar
        def _(act):
            a = nc.scalar.activation
            for t in range(TT):
                act.wait_ge(x_loaded[t // 4], 16)
                if t:
                    act.wait_ge(s["sqs_done"], t)
                a(sq[:, 0:DM], part[:, t, :], ACT.Square, accum_out=ssq0[:, t:t + 1]).then_inc(s["sqs_done"], 1)
            act.wait_ge(s["params_loaded"], 16 * 8)
            act.wait_ge(s["dtw_loaded"], 16)
            a(wo_hi[:, 0, :], wo_raw[:, 0, :], ACT.Copy).then_inc(s["dtw_hi"], 1)

            def split_high(g, idx):
                if not w_exists(g, idx):
                    return
                wait(act, w_loaded[idx % 3], 16 * (WT // 3), g, 16 * (idx // 3 + 1))
                wait(act, s["w_used"], WT, g, idx - 2)
                a(w_hi[:, idx % 3, :], w_raw[:, idx % 3, :], ACT.Copy).then_inc(s["w_high"], 1)

            split_high(0, 0)
            split_high(0, 1)
            for k in range(KT):
                for r, n in ((0, 4), (1, 3)):
                    i = 2 * k + r
                    act.wait_ge(s["hT_done"], i + 1)
                    a(h_hi[:, k, r * 512:r * 512 + n * P], [proj[0], proj[1], yt, ob][i // 2][:, i % 2, 0:n * P],
                      ACT.Copy, scale=norm_w[:, k:k + 1]).then_inc(s["h_evac_hi"], 1)
            act.wait_ge(s["dt_proj"], 1)
            a(seqs(yg[:, 0, :]), bank_seqs(proj[1]), ACT.Identity,
              bias=dt_bias[:, 0:1]).then_inc(s["dt_act"], 1)
            act.wait_ge(s["dt_act"], 1)
            a(yg[:, 1, :], yg[:, 0, :], ACT.Abs).then_inc(s["dt_act"], 1)
            act.wait_ge(s["dt_act"], 2)
            a(yg[:, 1, :], yg[:, 1, :], ACT.Exp, scale=-1.0).then_inc(s["dt_act"], 1)
            a(a_exp[:], a_log[:], ACT.Exp).then_inc(s["dt_act"], 1)
            act.wait_ge(s["dt_act"], 4)
            a(yg[:, 1, :], yg[:, 1, :], ACT.Ln, bias=1.0).then_inc(s["dt_act"], 1)
            def dt_token_major():
                for i in range(4):
                    act.wait_ge(s["cst_done"], i + 1)
                    dst = (cs_j if i < 2 else dt_j)[:, 4 * (i % 2):4 * (i % 2) + 4, :]
                    a(dst, [yt, ob][i // 2][:, i % 2, :].rearrange("p (q h) -> p q h", q=4),
                      ACT.Copy).then_inc(s["cst_evac"], 1)

            def first_tap(g, idx, col, m):
                wait(act, s["w_used"], WT, g, idx + 1)
                wait(act, s["silu_done"], 10, g, m - 1)
                a(seqs(conv[:, m % 2, :]), bank_seqs(proj[idx % 2]), ACT.Identity, bias=conv_b[:, bass.ds(col, 1)],
                  scale=conv_w[:, bass.ds(col, 1), TAPS - 1]).then_inc(s["tap0_done"], 1)

            def silu(g, m, dst):
                wait(act, s["conv_tap"], 30, g, 3 * m + 3)
                if m < 2:
                    wait(act, s["cb_done"], 1, g, 0)
                a(real(dst), seqs(conv[:, m % 2, :]), ACT.Silu).then_inc(s["silu_done"], 1)

            def silu_gate(g, c):
                wait(act, s["w_used"], WT, g, 4 + 2 * c)
                wait(act, s["p_done"], CT, g, c - 1)
                a(seqs(gate[:, c % 2, :]), bank_seqs(proj[1]), ACT.Silu).then_inc(s["gate_done"], 1)

            def half_free(g, c):
                if 0 <= c < 4:
                    wait(act, s["outb_done"], TT, g, 0)
                else:
                    wait(act, s["outa_done"], TT, g, TT if c >= 4 else 0)

            def y_high(g, c):
                if not within(g, c):
                    return
                wait(act, s["p_done"], CT, g, c + 1)
                half_free(g, c)
                a(y_hi[:, c % 4, :], yg[:, c % 2, :], ACT.Copy).then_inc(s["y_high"], 1)

            def squares(g, c):
                if not within(g, c):
                    return
                if c % CT == 0:
                    wait(act, s["ss_done"], 1, g, 0)
                    a(sqsum[:], yg[:, c % 2, :], ACT.Square).then_inc(s["sq_done"], 1)
                else:
                    wait(act, s["sqsum_done"], 7, g, c - 1 if c > 0 else c)
                    a(sq[:], yg[:, c % 2, :], ACT.Square).then_inc(s["sq_done"], 1)

            def wo_high(g, c):
                if not within(g, c):
                    return
                wait(act, wo_loaded[c % 2], 64, g, 16 * (c // 2 + 1))
                half_free(g, c)
                a(wo_hi[:, c % 4, :], wo_raw[:, c % 2, :], ACT.Copy,
                  scale=gnorm[:, bass.ds(g * CT + c, 1)]).then_inc(s["wo_high"], 1)

            def distance(g, c):
                if not within(g, c):
                    return
                wait(act, s["d_done"], CT, g, c + 1)
                a(decay[:, c % 4, :], decay[:, c % 4, :], ACT.Abs).then_inc(s["abs_done"], 1)

            def exps(g, lo, hi):
                for c in range(lo, hi):
                    wait(act, s["abs_done"], CT, g, c + 1)
                    a(decay[:, c % 4, :], decay[:, c % 4, :], ACT.Exp, scale=-1.0).then_inc(s["exp_done"], 1)

            def group(g, steps=CT):
                live = has_group(g)
                first = isinstance(g, int) and g == 0
                for st in range(steps):
                    if not (first and st == 0):
                        distance(g, st + 2)
                    exp_step = live and st % 4 == 1
                    if exp_step:
                        exps(g, st - 1, st)
                    y_high(g, st - 2)
                    if exp_step:
                        exps(g, st, st + 1)
                    if not live and st == 0:
                        wo_high(g, -2)
                        wo_high(g, -1)
                    squares(g, st - 2)
                    if live:
                        if st == 0:
                            first_tap(g, 0, g + GROUPS * CT, 0)
                            wo_high(g, -2)
                            split_high(g, 2)
                            split_high(g, 3)
                            first_tap(g, 1, g + GROUPS * CT + GROUPS, 1)
                            silu(g, 0, bmat[:])
                            split_high(g, 4)
                            silu(g, 1, cmat[:])
                        else:
                            split_high(g, 4 + 2 * st)
                            wo_high(g, st - 2)
                        first_tap(g, 2 + 2 * st, g * CT + st, 2 + st)
                        if first and st == 0:
                            dt_token_major()
                        if exp_step:
                            exps(g, st + 1, st + 3)
                        split_high(g, 5 + 2 * st)
                        wait(act, s["yres_done"], CT, g, st - 1)
                        silu(g, 2 + st, hid[:, st % 2, :])
                        silu_gate(g, st)
                        if first and st == 0:
                            for c in range(3):
                                distance(0, c)
                        if st == 5:
                            if first:
                                act.wait_ge(s["cs_stored"], 32)
                            for t in range(TT):
                                wait(act, s["outa_done"], TT, g, t + 1)
                                wait(act, s["sum_done"], TT, g, 0)
                                a(part[:, t, :], ob[:, t % 2, :], ACT.Copy).then_inc(s["outa_evac"], 1)
            over_groups(act, group)
            group(GROUPS, 2)
            def first_norm(t):
                act.wait_ge(s["ln1_rstd"], t + 1)
                a(acc[:, t, :], acc[:, t, :], ACT.Identity, bias=shift1[:, t:t + 1],
                  scale=rstd1[:, t:t + 1]).then_inc(s["x1_set"], 1)

            def transposed_keys(n, u):
                for i in range(0, 24, 2):
                    if isinstance(n, int) and (n, u, i) == (0, 0, 2):
                        first_norm(TT - 1)
                    dt, q, j = i // 6, i % 6 // 3, i % 3
                    wait(act, s["k_tr"], 48, n, 24 * u + i + 1)
                    if i % 6 == 0:
                        wait(act, s["s_mm"], 8, n, 4 * u + dt - 1)
                    a(keysT[:, dt % 2, q, 4 * KP * j:4 * KP * (j + 1)], kt_bank[0][:, 0:4 * KP],
                      ACT.Copy).then_inc(s["kev_act"], 1)

            def router_exp(n, u):
                wait(act, s["lg_done"], 2, n, u + 1)
                a(S["le"], S["lg"], ACT.Exp, bias=S["nlm"], accum_out=S["lsum"]).then_inc(s["le_done"], 1)

            def pairs(n):
                for u in range(2):
                    transposed_keys(n, u)
                    wait(act, s["nmax_done"], 2, n, u + 1)
                    wait(act, s["pT_tr"], 6, n, 3 * u)
                    wait(act, s["z2_done"], 2, n, u)
                    a(probs[:].rearrange("p (c n) -> p c n", c=3), scores, ACT.Exp, bias=S["nmax"],
                      accum_out=S["esum"]).then_inc(s["exps_done"], 1)
                    if pair_exists(n, u - 1):
                        router_exp(n, u - 1)
            for t in range(TT - 1):
                first_norm(t)
            over_pairs(act, pairs)
            router_exp(PAIRS // 2, -1)

        @block.vector
        def _(dve):
            v = nc.vector
            for i, (lo, hi) in enumerate(((0, 4), (4, TT))):
                dve.wait_ge(s["sqs_done"], hi)
                v.tensor_scalar(ms0[:, lo:hi], ssq0[:, lo:hi], 1.0 / DM, RMS_EPS, ALU.mult,
                                ALU.add).then_inc(s["ms0_set"], 1)
                dve.wait_ge(s["r0_set"], i + 1)
                for t in range(lo, hi):
                    v.tensor_scalar(part[:, t, :], part[:, t, :], r0[:, t:t + 1], None,
                                    ALU.mult).then_inc(s["h_scaled"], 1)
            v.memset(hid[:].rearrange("p a n -> p (a n)"), 0.0)
            for k in range(KT):
                for r, n in ((0, 4), (1, 3)):
                    i = 2 * k + r
                    dve.wait_ge(s["h_evac_hi"], i + 1)
                    v.scalar_tensor_tensor(out=h_lo[:, k, r * 512:r * 512 + n * P],
                                           in0=[proj[0], proj[1], yt, ob][i // 2][:, i % 2, 0:n * P],
                                           scalar=norm_w[:, k:k + 1],
                                           in1=h_hi[:, k, r * 512:r * 512 + n * P].bitcast(f32),
                                           op0=ALU.mult, op1=ALU.subtract).then_inc(s["h_evac_lo"], 1)
            keep = sqsum[:]
            v.memset(keep, 1.0).then_inc(s["dt_dve"], 1)
            dve.wait_ge(s["dt_dve"], 1)
            v.memset(keep.rearrange("p (b i) -> p b i", i=LEN)[:, :, 0:1], 0.0)
            dve.wait_ge(s["hT_done"], 8)
            v.memset(spare[:, 0:2 * SEQS * PAD], 0.0).then_inc(s["dt_dve"], 1)
            dve.wait_ge(s["dt_act"], 5)
            dve.wait_ge(s["dt_dve"], 2)
            v.scalar_tensor_tensor(out=real(dt_all), in0=seqs(yg[:, 0, :]), scalar=0.0,
                                   in1=seqs(yg[:, 1, :]), op0=ALU.max, op1=ALU.add).then_inc(s["dt_dve"], 1)
            dve.wait_ge(s["dt_dve"], 3)
            v.tensor_scalar(seqs(yg[:, 0, :]), real(dt_all), a_exp[:, 0:1], -1.0, ALU.mult,
                            ALU.mult).then_inc(s["dt_dve"], 1)
            dve.wait_ge(s["dt_dve"], 4)
            v.tensor_tensor_scan(sq[:], keep, yg[:, 0, :], 0.0, ALU.mult, ALU.add).then_inc(s["dt_dve"], 1)
            dve.wait_ge(s["dt_dve"], 5)
            v.tensor_copy(real(cs_all), seqs(sq[:])).then_inc(s["dt_dve"], 1)

            def taps(g, idx, col, m):
                dst, src = seqs(conv[:, m % 2, :]), bank_seqs(proj[idx % 2])
                for sh in range(1, TAPS):
                    if sh == 1:
                        wait(dve, s["tap0_done"], 10, g, m + 1)
                    else:
                        wait(dve, s["conv_tap"], 30, g, 3 * m + sh - 1)
                    v.scalar_tensor_tensor(out=dst[:, :, sh:LEN], in0=src[:, :, 0:LEN - sh],
                                           scalar=conv_w[:, bass.ds(col, 1), TAPS - 1 - sh],
                                           in1=dst[:, :, sh:LEN], op0=ALU.mult,
                                           op1=ALU.add).then_inc(s["conv_tap"], 1)

            def add_skip(g, c):
                if not within(g, c):
                    return
                wait(dve, s["y_done"], CT, g, c + 1)
                wait(dve, s["y_low"], CT, g, c - 1)
                wait(dve, s["sq_done"], CT, g, c - 1)
                v.scalar_tensor_tensor(out=seqs(yg[:, c % 2, :]), in0=real(hid[:, c % 2, :]),
                                       scalar=skip[:, bass.ds(g * CT + c, 1)], in1=bank_seqs(yt),
                                       op0=ALU.mult, op1=ALU.add).then_inc(s["yres_done"], 1)

            def multiply_gate(g, c):
                if not within(g, c):
                    return
                wait(dve, s["gate_done"], CT, g, c + 1)
                wait(dve, s["yres_done"], CT, g, c + 1)
                v.tensor_tensor(yg[:, c % 2, :], yg[:, c % 2, :], gate[:, c % 2, :],
                                ALU.mult).then_inc(s["p_done"], 1)

            def wo_low(g, c):
                if not within(g, c):
                    return
                wait(dve, s["wo_high"], CT, g, c + 1)
                v.scalar_tensor_tensor(out=wo_lo[:, c % 4, :], in0=wo_raw[:, c % 2, :],
                                       scalar=gnorm[:, bass.ds(g * CT + c, 1)],
                                       in1=wo_hi[:, c % 4, :].bitcast(f32), op0=ALU.mult,
                                       op1=ALU.subtract).then_inc(s["wo_low"], 1)

            def scale_hid(g, c):
                if not within(g, c):
                    return
                for r in range(2):
                    wait(dve, s["t_done"], 2 * CT, g, 2 * c + r + 1)
                    v.tensor_tensor(
                        hd_dt[:, 4 * r:4 * r + 4, :].rearrange("p q (h d) -> p q h d", h=2),
                        yt[:, r, :].rearrange("p (q h d) -> p q h d", q=4, h=2),
                        bc(dt_j[:, 4 * r:4 * r + 4, bass.ds(g * 16 + 2 * c, 2)], 3, HD),
                        ALU.mult).then_inc(s["hd_done"], 1)

            def differences(g, c):
                if not within(g, c):
                    return
                wait(dve, cs_loaded[c % 4], 64, g, 32 * (c // 4 + 1))
                t = decay[:, c % 4, :].rearrange("p (h q i) -> p h q i", h=2, i=LEN)
                v.tensor_tensor(t, t, bc(cs_j[:, :, bass.ds(g * 16 + 2 * c, 2)].rearrange("p q h -> p h q"), 3, LEN),
                                ALU.subtract).then_inc(s["d_done"], 1)

            def mix_high(g, c):
                if not within(g, c):
                    return
                wait(dve, s["exp_done"], CT, g, c + 1)
                wait(dve, s["y_done"], CT, g, c)
                wait(dve, s["cbm_done"], 1, g, 1 if c >= 0 else 0)
                v.scalar_tensor_tensor(
                    out=mixw[PAD:P, :, :, LEN:2 * LEN],
                    in0=decay[PAD:P, c % 4, :].rearrange("p (h q i) -> p h q i", h=2, i=LEN), scalar=1.0,
                    in1=bc(cbm[PAD:P, :, :], 1, 2), op0=ALU.mult, op1=ALU.mult).then_inc(s["m_hi_done"], 1)

            def mask_cb(g):
                wait(dve, s["m_lo_done"], CT, g, 0)
                wait(dve, s["m_hi_done"], CT, g, 0)
                wait(dve, s["cb_done"], 1, g, 1)
                v.tensor_tensor(cbm[:], ob[:, 0, 0:PAIRS * LEN].rearrange("p (q i) -> p q i", i=LEN),
                                bc(causal[:], 1, PAIRS), ALU.mult).then_inc(s["cbm_done"], 1)

            def group_squares(g):
                wait(dve, s["ss_done"], 1, g, 0)
                v.tensor_tensor(picked[:], ob[:, 0, 0:TT * SUB].rearrange("p (t a) -> p t a", a=SUB),
                                bc(own[:], 1, TT), ALU.mult).then_inc(s["ss_picked"], 1)
                wait(dve, s["ss_picked"], 1, g, 0)
                v.tensor_reduce(ssq[:], picked[:], AX.X, ALU.add).then_inc(s["ss_summed"], 1)
                wait(dve, s["ss_summed"], 1, g, 0)
                v.tensor_scalar(ms[:], ssq[:], 1.0 / (CT * P), RMS_EPS, ALU.mult, ALU.add).then_inc(s["ms_done"], 1)

            def add_output(g, t):
                wait(dve, s["outb_done"], TT, g, t - TT + 1)
                if t == 0:
                    if isinstance(g, int) and g == 1:
                        dve.wait_ge(s["residual_set"], 1)
                    wait(dve, s["outa_evac"], TT, g, 0)
                    wait(dve, s["rg_done"], 1, g, 0)
                v.tensor_tensor(part[:, t, :], ob[:, (t + 1) % 2, :], part[:, t, :],
                                ALU.add).then_inc(s["psum_added"], 1)
                wait(dve, s["psum_added"], TT, g, t - TT + 1)
                v.scalar_tensor_tensor(out=acc[:, t, :], in0=part[:, t, :], scalar=rg[:, t:t + 1],
                                       in1=acc[:, t, :], op0=ALU.mult, op1=ALU.add).then_inc(s["sum_done"], 1)

            dve.wait_ge(s["zeroed"], 1)
            v.tensor_reduce(own[:], ident[:].rearrange("p (i a) -> p a i", a=SUB), AX.X, ALU.add)
            v.tensor_copy(causal[PAD:P, :], causal_hi[PAD:P, :]).then_inc(s["dstep"], 1)
            dve.wait_ge(s["dstep"], 1)

            def norm1_stats(t):
                dve.wait_ge(s["sum_done"], (GROUPS - 1) * TT + t + 1)
                v.bn_stats(stats[:], acc[:, t, :]).then_inc(s["ln1_step"], 1)
                dve.wait_ge(s["ln1_step"], 2 * t + 1)
                v.bn_aggr(mv1[:, t, :], stats[:]).then_inc(s["ln1_step"], 1)
                dve.wait_ge(s["ln1_step"], 2 * t + 2)
                v.tensor_scalar(var1[:, t:t + 1], mv1[:, t, 1:2], LN_EPS, None, ALU.add).then_inc(s["ln1_var"], 1)
                v.tensor_scalar(nmean1[:, t:t + 1], mv1[:, t, 0:1], -1.0, None, ALU.mult).then_inc(s["ln1_var"], 1)

            def group(g, steps=CT):
                live = has_group(g)
                first = isinstance(g, int) and g == 0
                for st in range(steps):
                    add_skip(g, st - 2)
                    if live:
                        multiply_gate(g, st - 2)
                    mix_high(g, st - 1)
                    if not live:
                        scale_hid(g, st - 1)
                        multiply_gate(g, st - 2)
                        if st == 0:
                            wo_low(g, -2)
                            wo_low(g, -1)
                    if live and st == 0:
                        taps(g, 0, g + GROUPS * CT, 0)
                        taps(g, 1, g + GROUPS * CT + GROUPS, 1)
                    if live:
                        scale_hid(g, st - 1)
                        taps(g, 2 + 2 * st, g * CT + st, 2 + st)
                        wo_low(g, st - 2)
                    if first and st == 0:
                        dve.wait_ge(s["cst_evac"], 4)
                        for c in range(3):
                            differences(0, c)
                    differences(g, st + 3)
                    if st == 1 and not first:
                        group_squares(g)
                        for t in range(TT):
                            add_output(g, t)
                            if not live:
                                norm1_stats(t)
                    if live and st == 0:
                        mask_cb(g)
            over_groups(dve, group)
            group(GROUPS, 2)

            NORM2, ROUTE, NORM3 = 2, 16, 3
            STEPS = 2 * (NORM2 + ROUTE + NORM3)

            def link(ins, n, cell):
                ins.then_inc(s["dstep"], 1)
                cell[0] += 1
                wait(dve, s["dstep"], STEPS, n, cell[0])

            def link_one(ins):
                ins.then_inc(s["stats_set"], 1)
                dve.wait_ge(s["stats_set"], 1)
                dve.sem_inc(s["stats_set"], -1)

            def queries(n, u):
                wait(dve, s["q_tr"], 2, n, u + 1)
                wait(dve, s["s_mm"], 8, n, 4 * u)
                v.tensor_copy(qT[:], misc.rearrange("p (k t) -> p k t", k=KT)).then_inc(s["q_evac"], 1)

            def transposed_keys(n, u, lo, hi):
                for i in range(2 * lo + 1, 2 * hi, 2):
                    dt, q, j = i // 6, i % 6 // 3, i % 3
                    wait(dve, s["k_tr"], 48, n, 24 * u + i + 1)
                    if i % 6 == 1:
                        wait(dve, s["s_mm"], 8, n, 4 * u + dt - 1)
                    v.tensor_copy(keysT[:, dt % 2, q, 4 * KP * j:4 * KP * (j + 1)],
                                  kt_bank[1][:, 0:4 * KP]).then_inc(s["kev_dve"], 1)

            def score_max(n, u):
                wait(dve, s["s_mm"], 8, n, 4 * u + 4)
                wait(dve, s["exps_done"], 2, n, u)
                v.tensor_reduce(S["nmax"], scores, AX.XY, ALU.max, negate=True).then_inc(s["nmax_done"], 1)

            def transposed_probs(n, u):
                for r in range(3):
                    wait(dve, s["pT_tr"], 6, n, 3 * u + r + 1)
                    if r == 0:
                        wait(dve, s["pv_done"], 2, n, u)
                    v.tensor_copy(probsT[0:KP, 4 * r:4 * r + 4, :],
                                  bank[0:KP, r, :].rearrange("p (j t) -> p j t", j=4)).then_inc(s["pT_evac"], 1)

            def norm2_sum(n, u, cell):
                wait(dve, s["exps_done"], 2, n, u + 1)
                link(v.reciprocal(S["rsum"], S["esum"]), n, cell)
                wait(dve, s["pv_done"], 2, n, u + 1)
                v.scalar_tensor_tensor(out=x2[:, u, :], in0=pv, scalar=S["rsum"], in1=x1p[:, u, :],
                                       op0=ALU.mult, op1=ALU.add).then_inc(s["z2_done"], 1)

            def norm2_stats(n, u, cell):
                wait(dve, s["z2_done"], 2, n, u + 1)
                link_one(v.bn_stats(S["st2"], x2[:, u % 2, :]))
                link(v.bn_aggr(S["mv2"], S["st2"]), n, cell)
                v.tensor_scalar(S["var2"], S["mv2"][:, 1:2], LN_EPS, None, ALU.add).then_inc(s["var2_done"], 1)

            def norm2_apply(n, u):
                wait(dve, s["rstd2_done"], 2, n, u + 1)
                v.tensor_scalar(x2[:, u % 2, :], x2[:, u % 2, :], S["mv2"][:, 0:1], S["rstd2"], ALU.subtract,
                                ALU.mult).then_inc(s["x2_done"], 1)

            def x2_transposed(n, u):
                wait(dve, s["x2_tr"], 2, n, u + 1)
                v.tensor_copy(x2T[:], misc.rearrange("p (k t) -> p k t", k=KT)).then_inc(s["x2_evac"], 1)

            def route(n, u, cell):
                wait(dve, s["route_done"], 2, n, u + 1)
                link(v.tensor_copy(S["lg"], misc[:, P:P + EXP]), n, cell)
                v.tensor_reduce(S["nlm"], S["lg"], AX.X, ALU.max, negate=True).then_inc(s["lg_done"], 1)
                wait(dve, s["le_done"], 2, n, u + 1)
                link(v.reciprocal(S["lr"], S["lsum"]), n, cell)
                link(v.tensor_scalar(S["pr"], S["le"], S["lr"], None, ALU.mult), n, cell)
                link(v.tensor_reduce(S["v1"], S["pr"], AX.X, ALU.max), n, cell)
                link(v.scalar_tensor_tensor(out=S["k1"], in0=S["pr"], scalar=S["v1"], in1=order[:],
                                            op0=ALU.is_equal, op1=ALU.mult), n, cell)
                link(v.tensor_reduce(S["km1"], S["k1"], AX.X, ALU.max), n, cell)
                link(v.tensor_scalar(S["oh1"], order[:], S["km1"], None, ALU.is_equal), n, cell)
                link(v.scalar_tensor_tensor(out=S["p2"], in0=S["oh1"], scalar=-4.0, in1=S["pr"], op0=ALU.mult,
                                            op1=ALU.add), n, cell)
                link(v.tensor_reduce(S["v2"], S["p2"], AX.X, ALU.max), n, cell)
                link(v.scalar_tensor_tensor(out=S["k2"], in0=S["p2"], scalar=S["v2"], in1=order[:],
                                            op0=ALU.is_equal, op1=ALU.mult), n, cell)
                link(v.tensor_reduce(S["km2"], S["k2"], AX.X, ALU.max), n, cell)
                link(v.scalar_tensor_tensor(out=S["sel"], in0=order[:], scalar=S["km2"], in1=S["oh1"],
                                            op0=ALU.is_equal, op1=ALU.add), n, cell)
                link(v.tensor_tensor(S["top"], S["sel"], S["pr"], ALU.mult), n, cell)
                link(v.tensor_reduce(S["tsum"], S["top"], AX.X, ALU.add), n, cell)
                link(v.reciprocal(S["tr"], S["tsum"]), n, cell)
                link(v.tensor_scalar(S["wgt"], S["top"], S["tr"], LORA_SCALE, ALU.mult, ALU.mult), n, cell)
                v.tensor_tensor(hw[:].rearrange("p (e r) -> p e r", r=RANK),
                                misc[:, 0:P].rearrange("p (e r) -> p e r", r=RANK), bc(S["wgt"], 2, RANK),
                                ALU.mult).then_inc(s["hw_done"], 1)

            def hw_transposed(n, u):
                wait(dve, s["hw_tr"], 2, n, u + 1)
                v.tensor_copy(hwT[:], misc[:, 0:P]).then_inc(s["hw_evac"], 1)

            def norm3_sum(n, u, cell):
                sl = u % 2
                wait(dve, s["ffn_done"], 2, n, u + 1)
                wait(dve, stored[sl], 32, n, 32 * (u // 2))
                link(v.tensor_tensor(z3[:, sl, :], ffn, x2[:, sl, :], ALU.add), n, cell)

            def norm3_bias(n, u, cell):
                sl = u % 2
                link(v.tensor_tensor(z3[:, sl, :], z3[:, sl, :], bias[:], ALU.add), n, cell)

            def norm3_stats(n, u, cell):
                link_one(v.bn_stats(S["st3"], z3[:, u % 2, :]))
                link(v.bn_aggr(S["mv3"], S["st3"]), n, cell)
                v.tensor_scalar(S["var3"], S["mv3"][:, 1:2], LN_EPS, None, ALU.add).then_inc(s["var3_done"], 1)

            def norm3_apply(n, u):
                sl = u % 2
                wait(dve, s["rstd3_done"], 2, n, u + 1)
                v.tensor_scalar(z3[:, sl, :], z3[:, sl, :], S["mv3"][:, 0:1], S["rstd3"], ALU.subtract,
                                ALU.mult).then_inc(s["out_ready"], 1)


            def pairs(n):
                cell = [1 if isinstance(n, int) and n == 0 else 1 - 1 - ROUTE - 2 * NORM3]
                for u in range(2):
                    before, before2 = pair_exists(n, u - 1), pair_exists(n, u - 2)
                    transposed_keys(n, u, 0, 3)
                    queries(n, u)
                    if before:
                        norm2_stats(n, u - 1, cell)
                    transposed_keys(n, u, 3, 4)
                    if before:
                        norm2_apply(n, u - 1)
                    transposed_keys(n, u, 4, 5)
                    if before2:
                        norm3_sum(n, u - 2, cell)
                    transposed_keys(n, u, 5, 6)
                    if before2:
                        if isinstance(n, int) and n == 1 and u == 0:
                            dve.wait_ge(s["ffn_loaded"], 64)
                        norm3_bias(n, u - 2, cell)
                    transposed_keys(n, u, 6, 7)
                    if before2:
                        norm3_stats(n, u - 2, cell)
                    transposed_keys(n, u, 7, 8)
                    if before2:
                        norm3_apply(n, u - 2)
                    transposed_keys(n, u, 8, 12)
                    if before:
                        x2_transposed(n, u - 1)
                    score_max(n, u)
                    transposed_probs(n, u)
                    if before:
                        route(n, u - 1, cell)
                        hw_transposed(n, u - 1)
                    norm2_sum(n, u, cell)
            over_pairs(dve, pairs)
            cell = [1 - 1 - ROUTE - 2 * NORM3]
            norm2_stats(PAIRS // 2, -1, cell)
            norm2_apply(PAIRS // 2, -1)
            norm3_sum(PAIRS // 2, -2, cell)
            norm3_bias(PAIRS // 2, -2, cell)
            norm3_stats(PAIRS // 2, -2, cell)
            norm3_apply(PAIRS // 2, -2)
            x2_transposed(PAIRS // 2, -1)
            route(PAIRS // 2, -1, cell)
            hw_transposed(PAIRS // 2, -1)
            norm3_sum(PAIRS // 2, -1, cell)
            norm3_bias(PAIRS // 2, -1, cell)
            norm3_stats(PAIRS // 2, -1, cell)
            norm3_apply(PAIRS // 2, -1)

        @block.tensor
        def _(pe):
            mm, tr = nc.tensor.matmul, nc.tensor.transpose
            pe.wait_ge(s["consts_set"], 1)
            for k in range(KT):
                for r, n in ((0, 4), (1, 3)):
                    i = 2 * k + r
                    for q in range(n):
                        t = 4 * r + q
                        pe.wait_ge(s["h_scaled"], t + 1)
                        last = tr([proj[0], proj[1], yt, ob][i // 2][:, i % 2, q * P:(q + 1) * P],
                                  part[:, t, k * P:(k + 1) * P], ident[:])
                    last.then_inc(s["hT_done"], 1)

            def product(out, hi, lo, as_scaled=False):
                for k in range(KT):
                    if as_scaled:
                        pe.wait_ge(s["h_evac_lo"], max(2 * k + 2, 4))
                    for i, (w, x) in enumerate(((hi, h_hi), (hi, h_lo), (lo, h_hi))):
                        for half in range(2):
                            place = out[:, half, :].rearrange("p (b i) -> p b i", i=PAD)[:, :, 0:LEN]
                            last = mm(place, w[:, k * P:(k + 1) * P],
                                      x[:, k, half * HALF:(half + 1) * HALF],
                                      start=(k == 0 and i == 0), stop=(k == KT - 1 and i == 2))
                return last

            pe.wait_ge(s["dtw_lo"], 1)
            product(proj[1], wo_hi[:, 0, :], wo_lo[:, 0, :], as_scaled=True).then_inc(s["dt_proj"], 1)

            def dt_token_major():
                pe.wait_ge(s["dt_dve"], 6)
                for i in range(4):
                    for q in range(4):
                        pair = 4 * (i % 2) + q
                        last = tr([yt, ob][i // 2][:, i % 2, q * P:(q + 1) * P],
                                  (cs_all, dt_all)[i // 2][:, pair * P:(pair + 1) * P], ident[:])
                    last.then_inc(s["cst_done"], 1)

            def project(g, idx):
                wait(pe, s["w_low"], WT, g, idx + 1)
                product(proj[idx % 2], w_hi[:, idx % 3, :], w_lo[:, idx % 3, :]).then_inc(s["w_used"], 1)

            def transpose_hid(g, c):
                if not within(g, c):
                    return
                wait(pe, s["silu_done"], 10, g, c + 3 if c >= 0 else c + 1)
                wait(pe, s["yres_done"], CT, g, c)
                for r in range(2):
                    for q in range(4):
                        pair = 4 * r + q
                        last = tr(yt[:, r, q * P:(q + 1) * P], hid[:, c % 2, pair * P:(pair + 1) * P], ident[:])
                    last.then_inc(s["t_done"], 1)

            def y_product(g, c):
                if not within(g, c):
                    return
                wait(pe, s["hd_done"], 2 * CT, g, 2 * c + 2)
                wait(pe, s["m_lo_done"], CT, g, c + 1)
                wait(pe, s["m_hi_done"], CT, g, c + 1)
                for pair in range(PAIRS):
                    for h in range(2):
                        place = yt[HD * h:HD * (h + 1), pair // 4, pair % 4 * P:(pair % 4 + 1) * P]
                        last = mm(place.rearrange("p (s i) -> p s i", i=PAD)[:, :, 0:LEN],
                                  hd_dt[:, pair, HD * h:HD * (h + 1)], mixw[:, h, pair, :], start=True, stop=True)
                last.then_inc(s["y_done"], 1)

            def cb_product(g):
                wait(pe, s["silu_done"], 10, g, 2)
                wait(pe, s["outa_evac"], TT, g, 0)
                if isinstance(g, int) and g == 0:
                    pe.wait_ge(s["cst_evac"], 4)
                for b in range(SEQS):
                    last = mm(ob[PAD * (b % 2):PAD * (b % 2 + 1), 0, b // 2 * LEN:(b // 2 + 1) * LEN],
                              bmat[:, b * PAD:(b + 1) * PAD], cmat[:, b * PAD:b * PAD + LEN], start=True, stop=True)
                last.then_inc(s["cb_done"], 1)

            def out_product(t, b, g, done):
                for c in range(4):
                    if t == 0 and c in (0, 3):
                        wait(pe, s["y_low"], CT, g, done - (c == 0))
                        wait(pe, s["wo_low"], CT, g, done - (c == 0))
                    tok = slice(t * P, (t + 1) * P)
                    for i, (y, w) in enumerate(((y_hi, wo_hi), (y_hi, wo_lo), (y_lo, wo_hi))):
                        last = mm(ob[:, b, :], y[:, c, tok], w[:, c, :], start=(c == 0 and i == 0),
                                  stop=(c == 3 and i == 2))
                return last

            def sum_squares(g):
                wait(pe, s["sqsum_done"], 7, g, 0)
                if has_group(g):
                    wait(pe, s["cbm_done"], 1, g, 1)
                for i in range(P // SUB):
                    last = mm(ob[SUB * i:SUB * (i + 1), 0, 0:TT * SUB].rearrange("p (t a) -> p t a", a=SUB),
                              ones[:], sqsum[:].rearrange("p (t i a) -> p i t a", t=TT, a=SUB)[:, i],
                              start=True, stop=True)
                last.then_inc(s["ss_done"], 1)

            def second_half(g):
                wait(pe, s["outa_evac"], TT, g, 0)
                if has_group(g):
                    sum_squares(g)
                for t in range(TT):
                    if t == 1:
                        wait(pe, s["ss_picked"], 1, g, 0)
                    elif t > 1:
                        wait(pe, s["psum_added"], TT, g, t - 1 - TT)
                    out_product(t, (t + 1) % 2, g, 0).then_inc(s["outb_done"], 1)
                    if t == 0 and not has_group(g):
                        sum_squares(g)

            def first_half(g):
                wait(pe, s["psum_added"], TT, g, 0)
                wait(pe, s["cbm_done"], 1, g, 1)
                for t in range(TT):
                    if t > 1:
                        wait(pe, s["outa_evac"], TT, g, t - 1)
                    out_product(t, t % 2, g, 4).then_inc(s["outa_done"], 1)

            def group(g, steps=CT):
                live = has_group(g)
                for st in range(steps):
                    if live and st == 0:
                        wait(pe, s["conv_tap"], 30, g, 0)
                        project(g, 0)
                        wait(pe, s["gate_done"], CT, g, 0)
                        if isinstance(g, int) and g == 0:
                            pe.wait_ge(s["dt_act"], 1)
                        project(g, 1)
                        if isinstance(g, int) and g == 0:
                            dt_token_major()
                    if st == 0:
                        transpose_hid(g, -1)
                    if live:
                        wait(pe, s["conv_tap"], 30, g, 3 * st + 6 if st else 3)
                        project(g, 2 + 2 * st)
                    if st:
                        transpose_hid(g, st - 1)
                    if live:
                        if st:
                            wait(pe, s["gate_done"], CT, g, st)
                        else:
                            wait(pe, s["conv_tap"], 30, g, 6)
                        project(g, 3 + 2 * st)
                    if live and st == 0:
                        cb_product(g)
                    y_product(g, st - 1)
                    if st == 1 and not (isinstance(g, int) and g == 0):
                        second_half(g)
                    if live and st == 5:
                        first_half(g)
            over_groups(pe, group)
            group(GROUPS, 2)

            def to_channels(src, done):
                for k in range(KT):
                    last = tr(misc[:, k * P:(k + 1) * P], src[:, k * P:(k + 1) * P], ident[:])
                last.then_inc(done, 1)

            def transpose_keys(n, u, dt, part_of):
                for i in range(6 * dt + 2 * part_of, 6 * dt + 2 * part_of + 2):
                    q, j0 = i % 6 // 3, 4 * (i % 3)
                    if i % 2:
                        wait(pe, s["kev_dve"], 24, n, 12 * u + i // 2)
                    else:
                        wait(pe, s["kev_act"], 24, n, 12 * u + i // 2)
                    for j in range(4):
                        last = tr(kt_bank[i % 2][:, j * KP:(j + 1) * KP],
                                  keys[0:KP, u, q, j0 + j, dt * P:(dt + 1) * P], ident[0:KP, 0:KP])
                    last.then_inc(s["k_tr"], 1)

            def score(n, u, dt, c):
                if c == 0:
                    wait(pe, s["kev_act"], 24, n, 12 * u + 3 * dt + 3)
                    wait(pe, s["kev_dve"], 24, n, 12 * u + 3 * dt + 3)
                    if dt == 0:
                        wait(pe, s["q_evac"], 2, n, u + 1)
                        wait(pe, s["exps_done"], 2, n, u)
                        wait(pe, s["pT_evac"], 6, n, 3 * u)
                for q in range(2):
                    last = mm(scores[PAD * q:PAD * (q + 1), c, :], qT[:, dt, PAD * q:PAD * (q + 1)],
                              keysT[:, dt % 2, q, c * 500:(c + 1) * 500], start=(dt == 0), stop=(dt == KT - 1))
                if c == 2:
                    last.then_inc(s["s_mm"], 1)

            def transpose_x2(n, u):
                if not (isinstance(n, int) and n == PAIRS // 2):
                    wait(pe, s["q_evac"], 2, n, u + 2)
                wait(pe, s["x2_done"], 2, n, u + 1)
                to_channels(x2[:, u % 2, :], s["x2_tr"])

            def feed_forward(n, u):
                wait(pe, s["x2_evac"], 2, n, u + 1)
                if isinstance(n, int) and n == 0:
                    pe.wait_ge(s["ffn_loaded"], 64)
                for k in range(KT):
                    last = mm(misc[:, 0:P + EXP], x2T[:, k, :], waT[:, k, :], start=(k == 0), stop=(k == KT - 1))
                last.then_inc(s["route_done"], 1)
                wait(pe, s["rstd3_done"], 2, n, u)
                for k in range(KT):
                    mm(ffn, x2T[:, k, :], wbT[:, k, :], start=(k == 0), stop=False)

            def transpose_hw(n, u):
                wait(pe, s["hw_done"], 2, n, u + 1)
                tr(misc[:, 0:P], hw[:], ident[:]).then_inc(s["hw_tr"], 1)

            def lora(n, u):
                wait(pe, s["hw_evac"], 2, n, u + 1)
                mm(ffn, hwT[:], wlb[:], start=False, stop=True).then_inc(s["ffn_done"], 1)

            def transpose_probs(n, u):
                wait(pe, s["exps_done"], 2, n, u + 1)
                for r in range(3):
                    for j in range(4):
                        key = (4 * r + j) * KP
                        last = tr(bank[0:KP, r, j * P:(j + 1) * P], probs[:, key:key + KP], ident[:])
                    last.then_inc(s["pT_tr"], 1)

            def values(n, u, r):
                if r == 0:
                    wait(pe, s["z2_done"], 2, n, u)
                wait(pe, s["pT_evac"], 6, n, 3 * u + r + 1)
                for j in range(4 * r, 4 * r + 4):
                    for q in range(2):
                        last = mm(pv[PAD * q:PAD * (q + 1), :], probsT[0:KP, j, PAD * q:PAD * (q + 1)],
                                  keys[0:KP, u, q, j, :], start=(j == 0), stop=(j == KJ - 1))
                if r == 2:
                    last.then_inc(s["pv_done"], 1)

            def pairs(n):
                for u in range(2):
                    before = pair_exists(n, u - 1)
                    wait(pe, keys_loaded[u], 64, n, 64)
                    for c in range(3):
                        transpose_keys(n, u, 0, c)
                    wait(pe, x1_loaded[u], 32, n, 32)
                    if isinstance(n, int) and n + u == 0:
                        pe.wait_ge(s["psum_added"], GROUPS * TT)
                    wait(pe, s["hw_evac"], 2, n, u - 1)
                    to_channels(x1p[:, u, :], s["q_tr"])
                    for dt in range(1, KT):
                        for c in range(3):
                            transpose_keys(n, u, dt, c)
                            score(n, u, dt - 1, c)
                    if before:
                        transpose_x2(n, u - 1)
                    for c in range(3):
                        score(n, u, KT - 1, c)
                    if before:
                        feed_forward(n, u - 1)
                    transpose_probs(n, u)
                    values(n, u, 0)
                    values(n, u, 1)
                    if before:
                        transpose_hw(n, u - 1)
                    values(n, u, 2)
                    if before:
                        lora(n, u - 1)
            over_pairs(pe, pairs)
            transpose_x2(PAIRS // 2, -1)
            feed_forward(PAIRS // 2, -1)
            transpose_hw(PAIRS // 2, -1)
            lora(PAIRS // 2, -1)


def layouts(inputs):
    import numpy as np

    def flat(name):
        return np.asarray(inputs[name])

    inner = HEADS * HD
    w = flat("L0_attn_in_proj_w")
    tiles = w[:2 * inner + 2 * GROUPS * P].reshape(-1, P, KT, P)
    gate, hid = tiles[:64], tiles[64:128]
    b, c = tiles[128:128 + GROUPS], tiles[128 + GROUPS:]
    order = []
    for g in range(GROUPS):
        order += [b[g], c[g]]
        for t in range(CT):
            order += [hid[g * CT + t], gate[g * CT + t]]
    w_in = np.stack(order).transpose(0, 3, 2, 1).reshape(GROUPS * WT, P, KT * P)
    w_dt = w[-HEADS:].reshape(HEADS, KT, P).transpose(2, 1, 0).reshape(P, KT * HEADS)
    w_base = flat("L0_ffn_W_base").reshape(DM, KT, P).transpose(2, 1, 0).reshape(P, KT * DM)
    a_rows = flat("L0_ffn_lora_A").reshape(EXP * RANK, DM)
    w_a = np.concatenate([a_rows, flat("L0_ffn_W_router")]).reshape(P + EXP, KT, P).transpose(2, 1, 0)
    return {
        "x": flat("x").reshape(TOK, DM),
        "context": flat("ctx_4096").reshape(SEQS, KP, KJ * DM),
        "w_in": w_in,
        "w_dt": w_dt,
        "w_out": flat("L0_attn_out_proj_w").T.reshape(GROUPS * CT, P, DM),
        "norm_w": flat("L0_attn_norm_w").reshape(KT, P).T,
        "conv_w": flat("L0_attn_conv_w").reshape(CONVS, P, TAPS).transpose(1, 0, 2).reshape(P, CONVS * TAPS),
        "conv_b": flat("L0_attn_conv_b").reshape(CONVS, P).T,
        "dt_bias": flat("L0_attn_dt_bias").reshape(HEADS, 1),
        "a_log": flat("L0_attn_A_log").reshape(HEADS, 1),
        "skip": flat("L0_attn_Dp").reshape(GROUPS * CT, 2).T,
        "gnorm": flat("L0_attn_gnorm_w").reshape(GROUPS * CT, P).T,
        "w_base": w_base,
        "b_base": flat("L0_ffn_b_base").reshape(1, DM),
        "w_a": w_a.reshape(P, KT * (P + EXP)),
        "w_b": flat("L0_ffn_lora_B").transpose(0, 2, 1).reshape(EXP * RANK, DM),
    }


def kernel(**inputs):
    import numpy as np
    import concourse.bacc as bacc
    from concourse import mybir as my
    from concourse.bass_utils import run_bass_kernel_spmd

    nc = bacc.Bacc("TRN2", target_bir_lowering=False, num_devices=1)
    arrays, access = {}, {}
    for name, value in layouts(inputs).items():
        value = np.ascontiguousarray(value)
        arrays[f"in_{name}"] = value
        access[name] = nc.dram_tensor(f"in_{name}", value.shape, my.dt.from_np(value.dtype), kind="ExternalInput").ap()
    access["out"] = nc.dram_tensor("out", (TOK, DM), my.dt.float32, kind="ExternalOutput").ap()
    layer_kernel(nc, access)
    result = run_bass_kernel_spmd(nc, [arrays], core_ids=[0])
    return result.results[0]["out"].reshape(SEQS, LEN, DM)
```
